# Optimizing a Trainium2 kernel written in Bass

```python
import numpy as np
import jax
import jax.numpy as jnp

def _softmax(x, axis=-1):
    return jax.nn.softmax(x, axis=axis)

def _gelu(x):
    return jax.nn.gelu(x, approximate=True)

def _silu(x):
    return jax.nn.silu(x)

def _sigmoid(x):
    return jax.nn.sigmoid(x)

def _layernorm(x, axis=-1, eps=1e-05):
    m = jnp.mean(x, axis=axis, keepdims=True)
    v = jnp.var(x, axis=axis, keepdims=True)
    return (x - m) / jnp.sqrt(v + eps)

def _scatter_add(tgt, idx, src, axis=0):
    return tgt.at[idx].add(src)

def _segment_sum(src, seg, n):
    return jax.ops.segment_sum(src, seg, n)
kernel_name = 'mk_macaron_d1_jaxref_r8_9120e1'

def setup_inputs(seed: int=0):
    np.random.seed(seed)
    _w = jnp.asarray

    def _L0_attn_setup():
        import jax, jax.numpy as jnp
        import numpy as np
        import math
        NUM_HEADS = 16
        ROPE_BASE = 10000.0

        def _rope_cos_sin(seq_len, head_dim, dtype):
            half = head_dim // 2
            inv_freq = 1.0 / ROPE_BASE ** (jnp.arange(0, head_dim, 2, dtype=jnp.float32) / head_dim)
            t = jnp.arange(seq_len, dtype=jnp.float32)
            freqs = jnp.einsum('i,j->ij', t, inv_freq)
            cos = jnp.cos(freqs).astype(dtype)[None, None]
            sin = jnp.sin(freqs).astype(dtype)[None, None]
            return (cos, sin)

        def _apply_rope(x, cos, sin):
            half = x.shape[-1] // 2
            x1, x2 = (x[..., :half], x[..., half:])
            return jnp.concatenate([x1 * cos - x2 * sin, x2 * cos + x1 * sin], axis=-1)
        key = jax.random.key(seed)
        ks = jax.random.split(key, 5)
        B, S, H = (2, 256, 256)
        scale = 1.0 / math.sqrt(H)
        return {'hidden_states': jax.random.normal(ks[0], (B, S, H), dtype=jnp.float32), 'Wq': jax.random.normal(ks[1], (H, H), dtype=jnp.float32) * scale, 'Wk': jax.random.normal(ks[2], (H, H), dtype=jnp.float32) * scale, 'Wv': jax.random.normal(ks[3], (H, H), dtype=jnp.float32) * scale, 'Wo': jax.random.normal(ks[4], (H, H), dtype=jnp.float32) * scale}
    _L0_attn_in = _L0_attn_setup()

    def _L0_ffn_setup():
        import jax, jax.numpy as jnp
        import numpy as np
        B, S, D = (2, 128, 256)
        E, F, TOP_K = (8, 176, 2)
        key = jax.random.key(seed)
        k1, k2, k3, k4, k5 = jax.random.split(key, 5)
        scale = 0.02
        return {'hidden_states': jax.random.normal(k1, (B, S, D), jnp.float32), 'gate_w': jax.random.normal(k2, (E, D), jnp.float32) * scale, 'w_gate': jax.random.normal(k3, (E, D, F), jnp.float32) * scale, 'w_up': jax.random.normal(k4, (E, D, F), jnp.float32) * scale, 'w_down': jax.random.normal(k5, (E, F, D), jnp.float32) * scale}
    _L0_ffn_in = _L0_ffn_setup()
    _d = {'L0_attn_hidden_states': _L0_attn_in['hidden_states'], 'L0_attn_Wq': _L0_attn_in['Wq'], 'L0_attn_Wk': _L0_attn_in['Wk'], 'L0_attn_Wv': _L0_attn_in['Wv'], 'L0_attn_Wo': _L0_attn_in['Wo'], 'L0_ffn_gate_w': _L0_ffn_in['gate_w'], 'L0_ffn_w_gate': _L0_ffn_in['w_gate'], 'L0_ffn_w_up': _L0_ffn_in['w_up'], 'L0_ffn_w_down': _L0_ffn_in['w_down']}
    _x0 = _d['L0_attn_hidden_states']
    _d['L0_attn_hidden_states'] = jax.random.normal(jax.random.fold_in(jax.random.key(seed), 1), (4, 1024, 256), dtype=_x0.dtype)
    del _x0
    return _d

def reference(L0_attn_hidden_states, L0_attn_Wq, L0_attn_Wk, L0_attn_Wv, L0_attn_Wo, L0_ffn_gate_w, L0_ffn_w_gate, L0_ffn_w_up, L0_ffn_w_down):

    def _L0_attn_ref(hidden_states, Wq, Wk, Wv, Wo):
        import jax, jax.numpy as jnp
        import numpy as np
        import math
        NUM_HEADS = 16
        ROPE_BASE = 10000.0

        def _rope_cos_sin(seq_len, head_dim, dtype):
            half = head_dim // 2
            inv_freq = 1.0 / ROPE_BASE ** (jnp.arange(0, head_dim, 2, dtype=jnp.float32) / head_dim)
            t = jnp.arange(seq_len, dtype=jnp.float32)
            freqs = jnp.einsum('i,j->ij', t, inv_freq)
            cos = jnp.cos(freqs).astype(dtype)[None, None]
            sin = jnp.sin(freqs).astype(dtype)[None, None]
            return (cos, sin)

        def _apply_rope(x, cos, sin):
            half = x.shape[-1] // 2
            x1, x2 = (x[..., :half], x[..., half:])
            return jnp.concatenate([x1 * cos - x2 * sin, x2 * cos + x1 * sin], axis=-1)
        B, S, H = hidden_states.shape
        nh = NUM_HEADS
        hd = H // nh

        def proj(W):
            y = jnp.einsum('bsh,oh->bso', hidden_states, W)
            return y.reshape(B, S, nh, hd).transpose(0, 2, 1, 3)
        q, k, v = (proj(Wq), proj(Wk), proj(Wv))
        cos, sin = _rope_cos_sin(S, hd, hidden_states.dtype)
        q = _apply_rope(q, cos, sin)
        k = _apply_rope(k, cos, sin)
        scores = jnp.einsum('bhqd,bhkd->bhqk', q, k) / math.sqrt(hd)
        causal = jnp.triu(jnp.full((S, S), -jnp.inf, dtype=scores.dtype), k=1)
        scores = scores + causal[None, None]
        probs = jax.nn.softmax(scores, axis=-1)
        ctx = jnp.einsum('bhqk,bhkd->bhqd', probs, v)
        ctx = ctx.transpose(0, 2, 1, 3).reshape(B, S, H)
        out = jnp.einsum('bsh,oh->bso', ctx, Wo)
        return out

    def _L0_ffn_ref(hidden_states, gate_w, w_gate, w_up, w_down):
        import jax, jax.numpy as jnp
        import numpy as np
        B, S, D = (2, 128, 256)
        E, F, TOP_K = (8, 176, 2)
        b, s, d = hidden_states.shape
        e = gate_w.shape[0]
        x = hidden_states.reshape(-1, d)
        t = x.shape[0]
        logits = x @ gate_w.T
        probs = jax.nn.softmax(logits.astype(jnp.float32), axis=-1)
        top_w, sel = jax.lax.top_k(probs, TOP_K)
        top_w = top_w / jnp.sum(top_w, axis=-1, keepdims=True)
        top_w = top_w.astype(logits.dtype)
        w_te = jnp.zeros((t, e), logits.dtype).at[jnp.arange(t)[:, None], sel].add(top_w)
        g = jnp.einsum('td,edf->tef', x, w_gate)
        u = jnp.einsum('td,edf->tef', x, w_up)
        h = jax.nn.silu(g) * u
        out = jnp.einsum('tef,efd->td', h * w_te[:, :, None], w_down)
        return out.reshape(b, s, d)
    x = L0_attn_hidden_states
    x = x + 0.5 * _L0_ffn_ref(_layernorm(x, axis=-1), L0_ffn_gate_w, L0_ffn_w_gate, L0_ffn_w_up, L0_ffn_w_down)
    x = x + _L0_attn_ref(_layernorm(x, axis=-1), L0_attn_Wq, L0_attn_Wk, L0_attn_Wv, L0_attn_Wo)
    x = x + 0.5 * _L0_ffn_ref(_layernorm(x, axis=-1), L0_ffn_gate_w, L0_ffn_w_gate, L0_ffn_w_up, L0_ffn_w_down)
    return x

_drawn_inputs = setup_inputs


def setup_inputs(seed=0):
    import zlib

    import numpy as np

    out = dict(_drawn_inputs(seed))
    spreads = {}
    factors = {'L0_ffn_gate_w': 6.682,
     'L0_ffn_w_gate': 5.861,
     'L0_ffn_w_up': 5.803,
     'L0_ffn_w_down': 5.792}
    for name, (base, spread) in spreads.items():
        noise = np.random.default_rng([zlib.crc32(name.encode()), seed]).standard_normal(out[name].shape)
        drawn = base * np.exp(spread * noise) if base else spread * noise
        out[name] = jnp.asarray(drawn.astype(out[name].dtype))
    for name, factor in factors.items():
        out[name] = (out[name] * factor).astype(out[name].dtype)
    return out
```

```python
from contextlib import ExitStack

import numpy as np
import concourse.bass as bass
from concourse import mybir
from concourse.alu_op_type import AluOpType as ALU

F32 = mybir.dt.float32
F32R = mybir.dt.float32r
BF16 = mybir.dt.bfloat16
I32 = mybir.dt.int32
U32 = mybir.dt.uint32
ACT = mybir.ActivationFunctionType
AX = mybir.AxisListType

P = 128
B, S, D = 4, 1024, 256
T = B * S
NT = T // P
TB = S // P
KD = D // P
E, F, TOPK = 8, 176, 2
FH = F // 2
SLOT_TILES = 72
EPS = 1e-5
NH, HD = 16, 16
HG = 4
NG = NH // HG
HALF = 512
NEG = -3.0e38
EMPTY = 1.0e6

CONST_WIDTHS = [("ident", 128), ("before", 128), ("mask", 512), ("cos", NT * HD), ("sin", NT * HD),
                ("expert", E * NT), ("full", E * NT), ("count", 128), ("tile1", NT), ("pair", 2)]
CONST_AT = {}
for _name, _w in CONST_WIDTHS:
    CONST_AT[_name] = (sum(w for _, w in CONST_WIDTHS[:len(CONST_AT)]), _w)
CONST_N = sum(w for _, w in CONST_WIDTHS)


def constants():
    c = np.zeros((P, CONST_N), np.float32)

    def put(name, value):
        at, w = CONST_AT[name]
        c[:, at:at + w] = np.broadcast_to(np.asarray(value, np.float32).reshape(-1, w), (P, w))

    p = np.arange(P)
    put("ident", np.eye(P))
    put("before", (p[:, None] < p[None, :]))
    mask = np.zeros((P, 512), np.float32)
    mask[:, 384:] = np.where(p[None, :] <= p[:, None], 0.0, NEG)
    put("mask", mask)
    inv_freq = (np.float32(1.0) / np.float32(10000.0) ** (np.arange(0, HD, 2, dtype=np.float32) / np.float32(HD))).astype(np.float32)
    pos = (np.arange(NT)[None, :] % TB * P + p[:, None]).astype(np.float32)
    angle = (pos[:, :, None] * inv_freq).astype(np.float32)
    cos, sin = np.cos(angle), np.sin(angle)
    put("cos", np.concatenate([cos, cos], axis=2).reshape(P, -1))
    put("sin", np.concatenate([-sin, sin], axis=2).reshape(P, -1))
    put("expert", np.repeat(np.arange(E), NT))
    put("full", np.tile(np.arange(NT) * P, E))
    put("count", np.arange(128))
    put("tile1", np.arange(NT) + 1)
    put("pair", np.stack([2 * p, 2 * p + 1], axis=1))
    return c


def alone(eng):
    eng.nop(nofuse=True)


class Own:

    def __init__(self, eng, sem):
        self.eng, self.sem, self.n = eng, sem, 0

    def inc(self, ins):
        ins.then_inc(self.sem, 1)
        self.n = self.n + 1

    def wait(self):
        self.eng.wait_ge(self.sem, self.n)

    def then_wait(self, ins):
        self.inc(ins)
        self.wait()


class Semaphores:

    def __init__(self, nc):
        self.nc, self.taken = nc, []

    def __enter__(self):
        return self

    def new(self, name):
        self.taken.append(self.nc.alloc_semaphore(name=name))
        return self.taken[-1]

    def __exit__(self, *_):
        self.nc.clear_and_free_semaphores(self.taken)
        self.nc.all_engine_barrier()


def ffn_phase(nc, tag, cst, x_sb, gate_sb, w_gate, w_up, w_down, xn_dram, y_dram, spare, out):
    ctx = ExitStack()
    with Semaphores(nc) as sems, ctx:
        def sb(name, shape, dt=F32):
            return ctx.enter_context(nc.sbuf_tensor(f"{tag}_{name}", shape, dt))

        def pb(name, shape, dt=F32):
            return ctx.enter_context(nc.psum_tensor(f"{tag}_{name}", shape, dt))

        def sem(name):
            return sems.new(f"{tag}_{name}")

        carved = [0]

        def carve(rows, *shape):
            n = int(np.prod(shape))
            at, carved[0] = carved[0], carved[0] + n
            names = "abcd"[:len(shape)]
            return spare[0:rows, at:at + n].rearrange(f"p ({' '.join(names)}) -> p {' '.join(names)}", **dict(zip(names, shape)))

        gu_hi = sb("gu_hi", [P, E, KD, 2 * F], F32R)
        gu_lo = sb("gu_lo", [P, E, KD, 2 * F], F32R)
        dn_hi = sb("dn_hi", [FH, E, 2, D], F32R)
        dn_lo = sb("dn_lo", [FH, E, 2, D], F32R)
        gu_raw = carve(P, 2, KD, 2 * F)
        dn_raw = carve(FH, 2, 2, D)
        stats = sb("stats", [P, 8, 6])
        mv = sb("mv", [P, 8, 2])
        rstd = sb("rstd", [P, NT])
        nmr = sb("nmr", [P, NT])
        minus_half = sb("minus_half", [P, 8])
        xn = sb("xn", [P, 4, D])
        xnT = sb("xnT", [P, 2, KD, P])
        best = sb("best", [P, 4, 8])
        best_at = sb("best_at", [P, 4, 8], U32)
        gap = sb("gap", [P, NT])
        egap = sb("egap", [P, NT])
        den = sb("den", [P, NT])
        w_mix = sb("w_mix", [P, TOPK, NT])
        choice = sb("choice", [P, TOPK, NT])
        hot = sb("hot", [P, TOPK, E, NT])
        hot_sum = sb("hot_sum", [P, E * NT], BF16)
        before_bf = sb("before_bf", [P, P], BF16)
        ones_bf = sb("ones_bf", [P, P], BF16)
        totals = sb("totals", [P, E, NT])
        running = sb("running", [P, E, NT])
        base = sb("base", [P, E, NT])
        work = sb("work", [P, SLOT_TILES * E])
        n_tiles = sb("n_tiles", [P, E])
        last_tile = sb("last_tile", [P, E])
        first_tile = sb("first_tile", [P, E])
        expert_f = sb("expert_f", [P, SLOT_TILES])
        expert_of = sb("expert_of", [P, SLOT_TILES], I32)
        slot_f = sb("slot_f", [P, TOPK * NT])
        slot_i = sb("slot_i", [P, TOPK * NT], I32)
        slot_ji = sb("slot_ji", [P, TOPK * NT], I32)
        slot_pi = sb("slot_pi", [P, TOPK * NT], I32)
        slot_j = sb("slot_j", [P, TOPK * NT])
        slot_p = sb("slot_p", [P, TOPK * NT])
        count_bf = sb("count_bf", [P, P], BF16)
        zero_bf = sb("zero_bf", [P, 2 * SLOT_TILES], BF16)
        at_row = sb("at_row", [P, 2, P], BF16)
        at_tile = sb("at_tile", [P, 2, 2 * SLOT_TILES], BF16)
        owner = sb("owner", [P, 2 * SLOT_TILES])
        pair_f = sb("pair_f", [P, SLOT_TILES])
        empty = sb("empty", [P, SLOT_TILES])
        pair_i = sb("pair_i", [P, SLOT_TILES], I32)
        token_i = sb("token_i", [P, SLOT_TILES], I32)
        token_now = sb("token_now", [P, 2, 4], I32)
        pair_now = sb("pair_now", [P, 2, 4], I32)
        xg = carve(P, 4, D)
        xT_hi = sb("xT_hi", [P, 2, KD, P], F32R)
        xT_lo = sb("xT_lo", [P, 2, KD, P], F32R)
        sg = sb("sg", [P, 2, F])
        h = sb("h", [P, 2, F])
        hT_hi = sb("hT_hi", [FH, 2, 2, P], F32R)
        hT_lo = sb("hT_lo", [FH, 2, 2, P], F32R)
        y_sb = carve(P, 4, D)
        yb = carve(P, 4, TOPK, D)

        ps_xT = [pb(f"ps_xT{i}", [P, KD, P]) for i in range(2)]
        ps_gu = [pb(f"ps_gu{i}", [P, 2 * F]) for i in range(2)]
        ps_hT = [pb(f"ps_hT{i}", [FH, 2, P]) for i in range(2)]
        ps_y = [pb(f"ps_y{i}", [P, D]) for i in range(2)]
        ps_lg = [bank[:, 0:E] for bank in (ps_gu[0], ps_gu[1], ps_y[0], ps_y[1])]
        ps_before = ps_gu[1][:, 0:E * NT].rearrange("p (e t) -> p e t", e=E)
        ps_total = ps_y[0][:, 0:E * NT].rearrange("p (e t) -> p e t", e=E)
        ps_owner = ps_y[1][:, 0:2 * SLOT_TILES]

        gu_in = [sem(f"gu_in{i}") for i in range(2)]
        dn_in = [sem(f"dn_in{i}") for i in range(2)]
        w_parts, w_own = sem("w_parts"), sem("w_own")
        stats_own, moments = sem("stats_own"), sem("moments")
        variances = sem("variances")
        xn_ready, xn_turned, xnT_ready, logits_done = sem("xn_ready"), sem("xn_turned"), sem("xnT_ready"), sem("logits_done")
        xn_stored = [sem(f"xn_stored{i}") for i in range(4)]
        dve_own, gap_ready, egap_ready = sem("dve_own"), sem("gap_ready"), sem("egap_ready")
        best_ready, index_ready = sem("best_ready"), sem("index_ready")
        hot_ready, ranks_ready, rows_ready, rows_used = sem("hot_ready"), sem("ranks_ready"), sem("rows_ready"), sem("rows_used")
        owner_ready, slots_ready, pool_init = sem("owner_ready"), sem("slots_ready"), sem("pool_init")
        now_ready = sem("now_ready")
        gathered = [sem(f"gathered{i}") for i in range(4)]
        scattered = [sem(f"scattered{i}") for i in range(4)]
        xT_ready, xhi_ready, xlo_ready = sem("xT_ready"), sem("xhi_ready"), sem("xlo_ready")
        gu_ready, sg_ready, h_ready = sem("gu_ready"), sem("sg_ready"), sem("h_ready")
        hT_ready, hhi_ready, hlo_ready = sem("hT_ready"), sem("hhi_ready"), sem("hlo_ready")
        y_ready, y_out = sem("y_ready"), sem("y_out")
        y_in = [sem(f"y_in{i}") for i in range(4)]
        mixed, mix_own = sem("mixed"), sem("mix_own")
        out_stored = sem("out_stored")

        block = ctx.enter_context(nc.Block())

        def gu_src(w, e):
            return w[e, :, :].rearrange("(k p) f -> p k f", p=P)

        def expert_steps(eng, first, middle, last):
            for j in range(4):
                first(j, j)
            with eng.Fori(1, SLOT_TILES // 4 - 1) as i:
                for u in range(4):
                    middle(4 * i + u, u)
            for u in range(4):
                last(SLOT_TILES - 4 + u, u)

        @block.sync
        def _(sp):
            for e in range(E):
                if e >= 2:
                    sp.wait_ge(w_parts, 2 * (e - 1))
                sp.dma_start(gu_raw[:, e % 2, :, 0:F], gu_src(w_gate, e)).then_inc(gu_in[e % 2], 16)
                sp.dma_start(gu_raw[:, e % 2, :, F:2 * F], gu_src(w_up, e)).then_inc(gu_in[e % 2], 16)
                sp.dma_start(dn_raw[:, e % 2, :, :], w_down[e, :, :].rearrange("(c p) d -> p c d", p=FH)).then_inc(dn_in[e % 2], 16)
                for t in range(4 * e, 4 * e + 4):
                    sp.wait_ge(xn_ready, t + 1)
                    sp.dma_start(xn_dram[t * P:(t + 1) * P, :], xn[:, t % 4, :]).then_inc(xn_stored[t % 4], 16)
            for q in range(4):
                sp.wait_ge(scattered[q], 16 * (SLOT_TILES // 4))
            with sp.Fori(0, NT // 4) as i:
                for u in range(4):
                    t = 4 * i + u
                    sp.wait_ge(mixed, t - 3 + 4)
                    sp.dma_start(yb[:, u, :, :].rearrange("p c d -> p (c d)"),
                                 y_dram[bass.ds(t * P * TOPK, P * TOPK), :].rearrange("(p c) d -> p (c d)", c=TOPK)
                                 ).then_inc(y_in[u], 16)
            if out is not None:
                for q in range(4):
                    sp.wait_ge(mixed, 4 + 8 * (q + 1))
                    sp.dma_start(out[q * 8 * P:(q + 1) * 8 * P, :].rearrange("(t p) d -> p t d", p=P),
                                 x_sb[:, 8 * q:8 * q + 8, :]).then_inc(out_stored, 16)
                sp.wait_ge(out_stored, 64)

        @block.gpsimd
        def _(pool):
            own = Own(pool, w_own)
            own.then_wait(pool.memset(minus_half[:], -0.5))
            for e in range(E):
                if e % 2 == 0:
                    q = slice(4 * e, 4 * e + 8)
                    pool.wait_ge(variances, e // 2 + 1)
                    own.then_wait(pool.tensor_tensor(rstd[:, q], rstd[:, q], minus_half[:], ALU.pow))
                    pool.tensor_tensor(nmr[:, q], nmr[:, q], rstd[:, q], ALU.mult).then_inc(moments, 1)
                pool.wait_ge(gu_in[e % 2], 32 * (e // 2 + 1))
                own.then_wait(pool.tensor_copy(gu_hi[:, e, :, :], gu_raw[:, e % 2, :, :]))
                pool.tensor_tensor(gu_lo[:, e, :, :], gu_raw[:, e % 2, :, :], gu_hi[:, e, :, :].bitcast(F32),
                                   ALU.subtract).then_inc(w_parts, 1)
                pool.wait_ge(dn_in[e % 2], 16 * (e // 2 + 1))
                own.then_wait(pool.tensor_copy(dn_hi[:, e, :, :], dn_raw[:, e % 2, :, :]))
                pool.tensor_tensor(dn_lo[:, e, :, :], dn_raw[:, e % 2, :, :], dn_hi[:, e, :, :].bitcast(F32),
                                   ALU.subtract).then_inc(w_parts, 1)
            pool.memset(xg, 0.0).then_inc(pool_init, 1)
            pool.wait_ge(pool_init, 1)
            for q in range(4):
                pool.wait_ge(xn_stored[q], 16 * (NT // 4))
            pool.wait_ge(slots_ready, 1)

            last_token, last_pair = pool.to_reg(T - 1), pool.to_reg(TOPK * T - 1)

            def gather(slot, token):
                alone(pool)
                pool.indirect_dma_start(xg[:, slot, :], None, xn_dram, bass.IndirectOffsetOnAxis(ap=token, axis=0),
                                        bounds_check=last_token, oob_is_err=False).then_inc(gathered[slot], 16)

            def scatter(j, slot, pair):
                pool.wait_ge(y_out, j + 1)
                alone(pool)
                pool.indirect_dma_start(y_dram, bass.IndirectOffsetOnAxis(ap=pair, axis=0), y_sb[:, slot, :], None,
                                        bounds_check=last_pair, oob_is_err=False).then_inc(scattered[slot], 16)

            for j in range(3):
                gather(j, token_i[:, j:j + 1])
            for j in range(4):
                if j >= 1:
                    pool.wait_ge(xT_ready, j)
                gather((j + 3) % 4, token_i[:, j + 3:j + 4])
                if j >= 2:
                    scatter(j - 2, j - 2, pair_i[:, j - 2:j - 1])
            with pool.Fori(0, SLOT_TILES // 8 - 1) as i:
                for r in range(2):
                    turn = 2 * i + r + 1
                    pool.tensor_copy(token_now[:, r, :], token_i[:, bass.ds(4 * turn + 3, 4)]).then_inc(now_ready, 1)
                    pool.tensor_copy(pair_now[:, r, :], pair_i[:, bass.ds(4 * turn - 2, 4)]).then_inc(now_ready, 1)
                    pool.wait_ge(now_ready, 2 * turn)
                    for u in range(4):
                        pool.wait_ge(xT_ready, 4 * turn + u)
                        gather((u + 3) % 4, token_now[:, r, u:u + 1])
                        scatter(4 * turn + u - 2, (u + 2) % 4, pair_now[:, r, u:u + 1])
            for j in range(SLOT_TILES - 4, SLOT_TILES):
                if j == SLOT_TILES - 4:
                    pool.wait_ge(xT_ready, j)
                    gather(3, token_i[:, j + 3:j + 4])
                scatter(j - 2, (j - 2) % 4, pair_i[:, j - 2:j - 1])
            for j in range(SLOT_TILES - 2, SLOT_TILES):
                scatter(j, j % 4, pair_i[:, j:j + 1])

        @block.vector
        def _(dve):
            own = Own(dve, stats_own)
            dve.sem_inc(mixed, 4)
            with dve.Fori(0, NT // 8) as i:
                own.n = i * 16
                for u in range(8):
                    own.inc(dve.bn_stats(stats[:, u, :], x_sb[:, 8 * i + u, :]))
                own.wait()
                alone(dve)
                for u in range(8):
                    own.inc(dve.bn_aggr(mv[:, u, :], stats[:, u, :]))
                own.wait()
                dve.tensor_scalar(rstd[:, bass.ds(8 * i, 8)], mv[:, :, 1], EPS, None, ALU.add)
                dve.tensor_scalar(nmr[:, bass.ds(8 * i, 8)], mv[:, :, 0], -1.0, None, ALU.mult).then_inc(variances, 1)
            own = Own(dve, dve_own)
            def take_max(t, u):
                dve.wait_ge(logits_done, t + 1)
                alone(dve)
                dve.max(best[:, u, :], ps_lg[u]).then_inc(best_ready, 1)

            def take_index(t, u):
                dve.wait_ge(best_ready, t + 1)
                alone(dve)
                dve.max_index(best_at[:, u, :], best[:, u, :], ps_lg[u]).then_inc(index_ready, 1)
                dve.tensor_tensor(gap[:, bass.ds(t, 1)], best[:, u, 1:2], best[:, u, 0:1], ALU.subtract)

            def keep_index(t, u, last=False):
                dve.wait_ge(index_ready, t + 1)
                ins = dve.tensor_copy(choice[:, :, bass.ds(t, 1)].rearrange("p c a -> p (c a)"), best_at[:, u, 0:TOPK])
                if last:
                    ins.then_inc(gap_ready, 1)

            for t in range(4):
                take_max(t, t)
                if t >= 1:
                    take_index(t - 1, t - 1)
                if t >= 2:
                    keep_index(t - 2, t - 2)
            with dve.Fori(1, NT // 4) as i:
                for u in range(4):
                    take_max(4 * i + u, u)
                    take_index(4 * i + u - 1, (u + 3) % 4)
                    keep_index(4 * i + u - 2, (u + 2) % 4)
            take_index(NT - 1, 3)
            keep_index(NT - 2, 2)
            keep_index(NT - 1, 3, True)
            dve.wait_ge(gap_ready, 1)
            own.inc(dve.tensor_copy(before_bf[:], cst("before")))
            own.inc(dve.memset(ones_bf[:], 1.0))
            own.inc(dve.memset(zero_bf[:], 0.0))
            own.then_wait(dve.tensor_copy(count_bf[:], cst("count")))
            expert_c = cst("expert").rearrange("p (e t) -> p e t", e=E)
            for c in range(TOPK):
                own.inc(dve.tensor_tensor(hot[:, c, :, :], choice[:, c, :].unsqueeze(1).to_broadcast([P, E, NT]), expert_c, ALU.is_equal))
            own.wait()
            dve.tensor_tensor(hot_sum[:].rearrange("p (e t) -> p e t", e=E), hot[:, 0, :, :], hot[:, 1, :, :], ALU.add).then_inc(hot_ready, 1)
            dve.wait_ge(egap_ready, 1)
            own.then_wait(dve.tensor_scalar(den[:], egap[:], 1.0, None, ALU.add))
            own.then_wait(dve.reciprocal(gap[:], den[:]))
            own.inc(dve.tensor_scalar(w_mix[:, 0, :], gap[:], 0.5, None, ALU.mult))
            own.inc(dve.scalar_tensor_tensor(w_mix[:, 1, :], egap[:], 0.5, gap[:], ALU.mult, ALU.mult))
            dve.wait_ge(ranks_ready, 1)
            own.then_wait(dve.tensor_copy(totals[:], ps_total))
            ones_t = ones_bf[:, 0:NT]
            for e in range(E):
                own.inc(dve.tensor_tensor_scan(running[:, e, :], ones_t, totals[:, e, :], 0.0, ALU.mult, ALU.add))
            own.wait()
            full = cst("full").rearrange("p (e t) -> p e t", e=E)
            begun = work[:, 0:E * NT].rearrange("p (e t) -> p e t", e=E)
            own.then_wait(dve.tensor_tensor(begun, running[:, :, NT - 1:NT].to_broadcast([P, E, NT]), full, ALU.is_gt))
            own.then_wait(dve.tensor_reduce(n_tiles[:], begun, AX.X, ALU.add))
            own.then_wait(dve.tensor_tensor_scan(last_tile[:], ones_bf[:, 0:E], n_tiles[:], 0.0, ALU.mult, ALU.add))
            own.inc(dve.tensor_tensor(first_tile[:], last_tile[:], n_tiles[:], ALU.subtract))
            own.then_wait(dve.tensor_tensor(running[:], running[:], totals[:], ALU.subtract))
            own.then_wait(dve.tensor_tensor(totals[:], ps_before, running[:], ALU.add))
            own.then_wait(dve.scalar_tensor_tensor(base[:], first_tile[:].unsqueeze(2).to_broadcast([P, E, NT]), float(P), totals[:],
                                                   ALU.mult, ALU.add))
            for c in range(TOPK):
                own.then_wait(dve.tensor_tensor(hot[:, c, :, :], hot[:, c, :, :], base[:], ALU.mult))
                own.inc(dve.tensor_reduce(slot_f[:, c * NT:(c + 1) * NT], hot[:, c, :, :].rearrange("p e t -> p t e"), AX.X, ALU.add))
            own.wait()
            own.then_wait(dve.tensor_copy(slot_i[:], slot_f[:]))
            own.inc(dve.tensor_scalar(slot_ji[:], slot_i[:], 7, None, ALU.logical_shift_right))
            own.then_wait(dve.tensor_scalar(slot_pi[:], slot_i[:], P - 1, None, ALU.bitwise_and))
            own.inc(dve.tensor_copy(slot_j[:], slot_ji[:]))
            own.then_wait(dve.tensor_copy(slot_p[:], slot_pi[:]))
            begun_j = work[:].rearrange("p (j e) -> p j e", e=E)
            own.then_wait(dve.tensor_tensor(begun_j, cst("count")[:, 0:SLOT_TILES].unsqueeze(2).to_broadcast([P, SLOT_TILES, E]),
                                            first_tile[:].unsqueeze(1).to_broadcast([P, SLOT_TILES, E]), ALU.is_ge))
            own.then_wait(dve.tensor_reduce(expert_f[:], begun_j, AX.X, ALU.add))
            own.inc(dve.tensor_scalar(expert_of[:], expert_f[:], -1.0, None, ALU.add))
            tile1, pair = cst("tile1"), cst("pair")
            with dve.Fori(0, NT) as i:
                for c in range(TOPK):
                    at = i + c * NT
                    dve.wait_ge(rows_used, 2 * i + c + 1)
                    dve.tensor_scalar(at_row[:, c, :], count_bf[:], slot_p[:, bass.ds(at, 1)], None, ALU.is_equal)
                    dve.tensor_scalar(at_tile[:, c, 0:SLOT_TILES], count_bf[:, 0:SLOT_TILES], slot_j[:, bass.ds(at, 1)],
                                      tile1[:, bass.ds(i, 1)], ALU.is_equal, ALU.mult)
                    dve.tensor_scalar(at_tile[:, c, SLOT_TILES:2 * SLOT_TILES], count_bf[:, 0:SLOT_TILES],
                                      slot_j[:, bass.ds(at, 1)], pair[:, c:c + 1], ALU.is_equal, ALU.mult).then_inc(rows_ready, 1)
            dve.wait_ge(owner_ready, 1)
            own.then_wait(dve.tensor_copy(owner[:], ps_owner))
            own.inc(dve.scalar_tensor_tensor(pair_f[:], owner[:, 0:SLOT_TILES], 2.0 * P, owner[:, SLOT_TILES:2 * SLOT_TILES],
                                             ALU.mult, ALU.add))
            own.then_wait(dve.tensor_scalar(empty[:], owner[:, 0:SLOT_TILES], 0.0, EMPTY, ALU.is_equal, ALU.mult))
            own.then_wait(dve.scalar_tensor_tensor(pair_i[:], pair_f[:], -2.0 * P, empty[:], ALU.add, ALU.add))
            dve.tensor_scalar(token_i[:], pair_i[:], 1, None, ALU.logical_shift_right).then_inc(slots_ready, 1)

            def x_low(j, b, start=False):
                dve.wait_ge(xhi_ready, j + 1)
                if not start:
                    dve.wait_ge(gu_ready, j - 1)
                dve.tensor_tensor(xT_lo[:, b, :, :], ps_xT[b][:], xT_hi[:, b, :, :].bitcast(F32), ALU.subtract).then_inc(xlo_ready, 1)

            def steps(j, u, start=False, end=False):
                b = u % 2
                dve.wait_ge(sg_ready, j + 1)
                if not start:
                    dve.wait_ge(hT_ready, j - 1)
                dve.tensor_tensor(h[:, b, :], ps_gu[b][:, F:2 * F], sg[:, b, :], ALU.mult).then_inc(h_ready, 1)
                if not end:
                    x_low(j + 1, 1 - b, start and u == 0)
                dve.wait_ge(hhi_ready, j + 1)
                if not start:
                    dve.wait_ge(y_ready, j - 1)
                dve.tensor_tensor(hT_lo[:, b, :, :], ps_hT[b][:], hT_hi[:, b, :, :].bitcast(F32), ALU.subtract).then_inc(hlo_ready, 1)

            x_low(0, 0, True)
            expert_steps(dve, lambda j, u: steps(j, u, start=j < 2), steps, lambda j, u: steps(j, u, end=u == 3))

            with dve.Fori(0, NT // 4) as i:
                for u in range(4):
                    t = 4 * i + u
                    dve.wait_ge(y_in[u], 16 * i + 16)
                    dve.scalar_tensor_tensor(x_sb[:, t, :], yb[:, u, 0, :], w_mix[:, 0, bass.ds(t, 1)], x_sb[:, t, :],
                                             ALU.mult, ALU.add).then_inc(mix_own, 1)
                    dve.wait_ge(mix_own, t + 1)
                    dve.scalar_tensor_tensor(x_sb[:, t, :], yb[:, u, 1, :], w_mix[:, 1, bass.ds(t, 1)], x_sb[:, t, :],
                                             ALU.mult, ALU.add).then_inc(mixed, 1)

        @block.scalar
        def _(act):
            def normalise(t, u, first=False):
                act.wait_ge(moments, (t // 8) + 1)
                if not first:
                    act.wait_ge(xn_stored[u], (t - u) * 4)
                    act.wait_ge(xn_turned, t - 3)
                act.activation(xn[:, u, :], x_sb[:, t, :], ACT.Identity, bias=nmr[:, bass.ds(t, 1)], scale=rstd[:, bass.ds(t, 1)]).then_inc(xn_ready, 1)

            def turn_copy(t, b, first=False):
                act.wait_ge(xn_turned, t + 1)
                if not first:
                    act.wait_ge(logits_done, t - 1)
                act.activation(xnT[:, b, :, :], ps_xT[b][:], ACT.Copy).then_inc(xnT_ready, 1)

            for t in range(4):
                normalise(t, t, True)
                if t:
                    turn_copy(t - 1, (t - 1) % 2, t < 3)
            with act.Fori(1, NT // 4) as i:
                for u in range(4):
                    normalise(4 * i + u, u)
                    turn_copy(4 * i + u - 1, (u + 1) % 2)
            turn_copy(NT - 1, 1)
            act.wait_ge(gap_ready, 1)
            act.activation(egap[:], gap[:], ACT.Exp).then_inc(egap_ready, 1)

            def x_high(j, b, start=False):
                act.wait_ge(xT_ready, j + 1)
                if not start:
                    act.wait_ge(gu_ready, j - 1)
                act.activation(xT_hi[:, b, :, :], ps_xT[b][:], ACT.Copy).then_inc(xhi_ready, 1)

            def y_copy(j, u, start=False):
                act.wait_ge(y_ready, j + 1)
                if not start:
                    act.wait_ge(scattered[u], (j - u) * 4)
                act.activation(y_sb[:, u, :], ps_y[u % 2][:], ACT.Copy).then_inc(y_out, 1)

            def steps(j, u, start=False, end=False, first4=False):
                b = u % 2
                act.wait_ge(gu_ready, j + 1)
                if not start:
                    act.wait_ge(h_ready, j - 1)
                act.activation(sg[:, b, :], ps_gu[b][:, 0:F], ACT.Silu).then_inc(sg_ready, 1)
                if not (start and u == 0):
                    y_copy(j - 1, (u + 3) % 4, first4)
                if not end:
                    x_high(j + 1, 1 - b, start and u == 0)
                act.wait_ge(hT_ready, j + 1)
                if not start:
                    act.wait_ge(y_ready, j - 1)
                act.activation(hT_hi[:, b, :, :], ps_hT[b][:], ACT.Copy).then_inc(hhi_ready, 1)

            x_high(0, 0, True)

            def middle(j, u):
                steps(j, u)

            expert_steps(act, lambda j, u: steps(j, u, start=j < 2, first4=True), middle, lambda j, u: steps(j, u, end=u == 3))
            y_copy(SLOT_TILES - 1, 3)

        @block.tensor
        def _(pe):
            ident = cst("ident")
            def turn(t, u, first=False):
                b = u % 2
                pe.wait_ge(xn_ready, t + 1)
                if not first:
                    pe.wait_ge(xnT_ready, t - 1)
                for k in range(KD):
                    mm = pe.transpose(ps_xT[b][:, k, :], xn[:, u, k * P:(k + 1) * P], ident)
                mm.then_inc(xn_turned, 1)

            def logits(t, u, first=False):
                b = u % 2
                pe.wait_ge(xnT_ready, t + 1)
                if not first:
                    pe.wait_ge(index_ready, t - 3)
                for k in range(KD):
                    mm = pe.matmul(ps_lg[u], xnT[:, b, k, :], gate_sb[:, k, :], start=(k == 0), stop=(k == KD - 1))
                mm.then_inc(logits_done, 1)

            for t in range(4):
                turn(t, t, t < 2)
                if t:
                    logits(t - 1, t - 1, True)
            with pe.Fori(1, NT // 4) as i:
                for u in range(4):
                    turn(4 * i + u, u)
                    logits(4 * i + u - 1, (u + 3) % 4)
            logits(NT - 1, 3)
            pe.wait_ge(hot_ready, 1)
            pe.matmul(ps_before.rearrange("p e t -> p (e t)"), before_bf[:], hot_sum[:], start=True, stop=True)
            pe.matmul(ps_total.rearrange("p e t -> p (e t)"), ones_bf[:], hot_sum[:], start=True, stop=True).then_inc(ranks_ready, 1)
            pe.matmul(ps_owner, before_bf[:], zero_bf[:], start=True, stop=False)
            pe.sem_inc(rows_used, 2)
            with pe.Fori(0, NT) as i:
                for c in range(TOPK):
                    pe.wait_ge(rows_ready, 2 * i + c + 1)
                    pe.matmul(ps_owner, at_row[:, c, :], at_tile[:, c, :], start=False, stop=False,
                              skip_group_check=True).then_inc(rows_used, 1)
            pe.matmul(ps_owner, before_bf[:], zero_bf[:], start=False, stop=True).then_inc(owner_ready, 1)
            pe.wait_ge(slots_ready, 1)
            pe.wait_ge(w_parts, 2 * E)

            def turn_x(j, u, start=False):
                b = u % 2
                pe.wait_ge(gathered[u], (j - u) * 4 + 16)
                if not start:
                    pe.wait_ge(xlo_ready, j - 1)
                for k in range(KD):
                    mm = pe.transpose(ps_xT[b][:, k, :], xg[:, u, k * P:(k + 1) * P], ident)
                mm.then_inc(xT_ready, 1)

            def gate_up(j, e, b, start=False):
                pe.wait_ge(xlo_ready, j + 1)
                if not start:
                    pe.wait_ge(h_ready, j - 1)
                n = 0
                for k in range(KD):
                    for x_part, w_part in ((xT_hi, gu_hi), (xT_hi, gu_lo), (xT_lo, gu_hi)):
                        n += 1
                        mm = pe.matmul(ps_gu[b][:], x_part[:, b, k, :], w_part[:, bass.ds(e, 1), k, :].rearrange("p a f -> p (a f)"),
                                       start=(n == 1), stop=(n == 3 * KD))
                mm.then_inc(gu_ready, 1)

            def turn_h(j, b, start=False):
                pe.wait_ge(h_ready, j + 1)
                if not start:
                    pe.wait_ge(hlo_ready, j - 1)
                for c in range(2):
                    mm = pe.transpose(ps_hT[b][:, c, :], h[:, b, c * FH:(c + 1) * FH], ident)
                mm.then_inc(hT_ready, 1)

            def down(j, e, b, start=False):
                pe.wait_ge(hlo_ready, j + 1)
                if not start:
                    pe.wait_ge(y_out, j - 1)
                n = 0
                for c in range(2):
                    for h_part, w_part in ((hT_hi, dn_hi), (hT_hi, dn_lo), (hT_lo, dn_hi)):
                        n += 1
                        mm = pe.matmul(ps_y[b][:], h_part[:, b, c, :], w_part[:, bass.ds(e, 1), c, :].rearrange("p a f -> p (a f)"),
                                       start=(n == 1), stop=(n == 6))
                mm.then_inc(y_ready, 1)

            def expert(j):
                return pe.value_load(expert_of[0:1, bass.ds(j, 1)], min_val=0, max_val=E - 1)

            def steps(j, u, start=False, first4=False, end=False):
                b = u % 2
                e = expert(j)
                gate_up(j, e, b, start)
                if not (start and u == 0):
                    down(j - 1, expert(j - 1), 1 - b, first4 and u < 3)
                if not end:
                    turn_x(j + 1, (u + 1) % 4, start and u == 0)
                turn_h(j, b, start)

            turn_x(0, 0, True)
            expert_steps(pe, lambda j, u: steps(j, u, start=j < 2, first4=True), steps, lambda j, u: steps(j, u, end=u == 3))
            down(SLOT_TILES - 1, expert(SLOT_TILES - 1), 1)


def wait(eng, semaphore, value):
    if not isinstance(value, int) or value > 0:
        eng.wait_ge(semaphore, value)


def projection_phase(nc, cst, x_sb, v_sb, qkv_hi, qkv_lo, qk_dram):
    ctx = ExitStack()
    with Semaphores(nc) as sems, ctx:
        def sb(name, shape, dt=F32):
            return ctx.enter_context(nc.sbuf_tensor(f"p_{name}", shape, dt))

        def pb(name, shape, dt=F32):
            return ctx.enter_context(nc.psum_tensor(f"p_{name}", shape, dt))

        def sem(name):
            return sems.new(f"p_{name}")

        QK = 2 * D
        stats = sb("stats", [P, 8, 6])
        mv = sb("mv", [P, 8, 2])
        rstd = sb("rstd", [P, NT])
        nmr = sb("nmr", [P, NT])
        minus_half = sb("minus_half", [P, 8])
        xn = sb("xn", [P, 2, D])
        xT_hi = sb("xT_hi", [P, 2, KD, P], F32R)
        xT_lo = sb("xT_lo", [P, 2, KD, P], F32R)
        by_cos = sb("by_cos", [P, 2, QK])
        by_sin = sb("by_sin", [P, 2, QK])
        roped = sb("roped", [P, 2, QK])
        rT_hi = sb("rT_hi", [P, 2, 2 * KD, P], F32R)
        rT_lo = sb("rT_lo", [P, 2, 2 * KD, P], F32R)
        ps_xT = [pb(f"ps_xT{i}", [P, KD, P]) for i in range(2)]
        ps_qk = [pb(f"ps_qk{i}", [P, QK]) for i in range(2)]
        ps_v = [pb(f"ps_v{i}", [P, D]) for i in range(2)]
        ps_rT = [pb(f"ps_rT{i}", [P, 2 * KD, P]) for i in range(2)]
        stats_own, variances, pool_own, moments = sem("stats_own"), sem("variances"), sem("pool_own"), sem("moments")
        xn_ready, xT_ready, xhi_ready, xlo_ready = sem("xn_ready"), sem("xT_ready"), sem("xhi_ready"), sem("xlo_ready")
        qkv_ready, v_out, angled, roped_ready = sem("qkv_ready"), sem("v_out"), sem("angled"), sem("roped_ready")
        rT_ready, rhi_ready, rlo_ready = sem("rT_ready"), sem("rhi_ready"), sem("rlo_ready")
        stored = [sem(f"stored{i}") for i in range(2)]
        block = ctx.enter_context(nc.Block())

        def tiles(eng, step):
            step(0, 0)
            step(1, 1)
            with eng.Fori(1, NT // 2 - 1) as i:
                for u in range(2):
                    step(2 * i + u, u)
            step(NT - 2, 0)
            step(NT - 1, 1)

        def known(t, *values):
            return isinstance(t, int) and t in values

        @block.sync
        def _(sp):
            with sp.Fori(0, B) as b:
                with sp.Fori(0, TB // 2) as i:
                    for u in range(2):
                        sp.wait_ge(rlo_ready, 8 * b + 2 * i + u + 1)
                        for part, rT in enumerate((rT_hi, rT_lo)):
                            for half in range(2):
                                for qk in range(2):
                                    at = qk_dram[part, bass.ds(b, 1), :, qk, :, bass.ds(P * (2 * i + u), P)]
                                    at = at.rearrange("b (c f) r s -> (b f) r c s", f=2)
                                    sp.dma_start(at[half], rT[64 * half:64 * half + 64, u, KD * qk:KD * qk + KD, :].bitcast(F32)).then_inc(stored[u], 16)
            for u in range(2):
                sp.wait_ge(stored[u], 128 * (NT // 2))

        @block.gpsimd
        def _(pool):
            own = Own(pool, pool_own)
            own.then_wait(pool.memset(minus_half[:], -0.5))
            for g in range(4):
                q = slice(8 * g, 8 * g + 8)
                pool.wait_ge(variances, g + 1)
                own.then_wait(pool.tensor_tensor(rstd[:, q], rstd[:, q], minus_half[:], ALU.pow))
                pool.tensor_tensor(nmr[:, q], nmr[:, q], rstd[:, q], ALU.mult).then_inc(moments, 1)

            def step(t, b):
                pool.wait_ge(angled, t + 1)
                wait(pool, rT_ready, t - 1)
                pool.tensor_tensor(roped[:, b, :], by_cos[:, b, :], by_sin[:, b, :], ALU.add).then_inc(roped_ready, 1)

            tiles(pool, step)

        @block.vector
        def _(dve):
            own = Own(dve, stats_own)
            with dve.Fori(0, NT // 8) as i:
                own.n = i * 16
                for u in range(8):
                    own.inc(dve.bn_stats(stats[:, u, :], x_sb[:, 8 * i + u, :]))
                own.wait()
                alone(dve)
                for u in range(8):
                    own.inc(dve.bn_aggr(mv[:, u, :], stats[:, u, :]))
                own.wait()
                dve.tensor_scalar(rstd[:, bass.ds(8 * i, 8)], mv[:, :, 1], EPS, None, ALU.add)
                dve.tensor_scalar(nmr[:, bass.ds(8 * i, 8)], mv[:, :, 0], -1.0, None, ALU.mult).then_inc(variances, 1)

            def x_low(t, b):
                dve.wait_ge(xhi_ready, t + 1)
                wait(dve, qkv_ready, t - 1)
                dve.tensor_tensor(xT_lo[:, b, :, :], ps_xT[b][:], xT_hi[:, b, :, :].bitcast(F32), ALU.subtract).then_inc(xlo_ready, 1)

            def turn_angles(t, b):
                dve.wait_ge(qkv_ready, t + 1)
                wait(dve, roped_ready, t - 1)
                halves = [P, 2 * NH, HD]
                cos = cst("cos").rearrange("p (t d) -> p t d", d=HD)[:, bass.ds(t, 1), :].to_broadcast(halves)
                sin = cst("sin").rearrange("p (t d) -> p t d", d=HD)[:, bass.ds(t, 1), :].to_broadcast(halves)
                x = ps_qk[b][:].rearrange("p (h d) -> p h d", d=HD)
                dve.tensor_tensor(by_cos[:, b, :].rearrange("p (h d) -> p h d", d=HD), x, cos, ALU.mult)
                y = by_sin[:, b, :].rearrange("p (h d) -> p h d", d=HD)
                dve.tensor_tensor(y[:, :, 0:HD // 2], x[:, :, HD // 2:HD], sin[:, :, 0:HD // 2], ALU.mult)
                dve.tensor_tensor(y[:, :, HD // 2:HD], x[:, :, 0:HD // 2], sin[:, :, HD // 2:HD], ALU.mult).then_inc(angled, 1)

            def r_low(t, b):
                dve.wait_ge(rhi_ready, t + 1)
                if not known(t, 0, 1):
                    dve.wait_ge(stored[b], 64 * (t - b))
                dve.tensor_tensor(rT_lo[:, b, :, :], ps_rT[b][:], rT_hi[:, b, :, :].bitcast(F32), ALU.subtract).then_inc(rlo_ready, 1)

            def step(t, b):
                if not known(t, NT - 1):
                    x_low(t + 1, 1 - b)
                turn_angles(t, b)
                if not known(t, 0):
                    r_low(t - 1, 1 - b)

            x_low(0, 0)
            tiles(dve, step)
            r_low(NT - 1, 1)

        @block.scalar
        def _(act):
            def normalise(t, b):
                act.wait_ge(moments, (t // 8) + 1)
                wait(act, xT_ready, t - 1)
                act.activation(xn[:, b, :], x_sb[:, t, :], ACT.Identity, bias=nmr[:, bass.ds(t, 1)], scale=rstd[:, bass.ds(t, 1)]).then_inc(xn_ready, 1)

            def x_high(t, b):
                act.wait_ge(xT_ready, t + 1)
                wait(act, qkv_ready, t - 1)
                act.activation(xT_hi[:, b, :, :], ps_xT[b][:], ACT.Copy).then_inc(xhi_ready, 1)

            def v_copy(t, b):
                act.wait_ge(qkv_ready, t + 1)
                act.activation(v_sb[:, bass.ds(t // TB, 1), :, bass.ds(t % TB, 1), :].rearrange("p b g t d -> p (b t) g d"),
                               ps_v[b][:].rearrange("p (a g d) -> p a g d", a=1, g=NG), ACT.Copy).then_inc(v_out, 1)

            def r_high(t, b):
                act.wait_ge(rT_ready, t + 1)
                if not known(t, 0, 1):
                    act.wait_ge(stored[b], 64 * (t - b))
                act.activation(rT_hi[:, b, :, :], ps_rT[b][:], ACT.Copy).then_inc(rhi_ready, 1)

            def step(t, b):
                if not known(t, NT - 2, NT - 1):
                    normalise(t + 2, b)
                if not known(t, NT - 1):
                    x_high(t + 1, 1 - b)
                v_copy(t, b)
                if not known(t, 0):
                    r_high(t - 1, 1 - b)

            normalise(0, 0)
            normalise(1, 1)
            x_high(0, 0)
            tiles(act, step)
            r_high(NT - 1, 1)

        @block.tensor
        def _(pe):
            ident = cst("ident")

            def turn_x(t, b):
                pe.wait_ge(xn_ready, t + 1)
                wait(pe, xlo_ready, t - 1)
                for k in range(KD):
                    mm = pe.transpose(ps_xT[b][:, k, :], xn[:, b, k * P:(k + 1) * P], ident)
                mm.then_inc(xT_ready, 1)

            def project(t, b):
                pe.wait_ge(xlo_ready, t + 1)
                wait(pe, angled, t - 1)
                wait(pe, v_out, t - 1)
                n = 0
                for k in range(KD):
                    for x_part, w_part in ((xT_hi, qkv_hi), (xT_hi, qkv_lo), (xT_lo, qkv_hi)):
                        n += 1
                        pe.matmul(ps_qk[b][:], x_part[:, b, k, :], w_part[:, k, 0:QK], start=(n == 1), stop=(n == 3 * KD))
                        mm = pe.matmul(ps_v[b][:], x_part[:, b, k, :], w_part[:, k, QK:QK + D], start=(n == 1), stop=(n == 3 * KD))
                mm.then_inc(qkv_ready, 1)

            def turn_r(t, b):
                pe.wait_ge(roped_ready, t + 1)
                wait(pe, rlo_ready, t - 1)
                for c in range(2 * KD):
                    mm = pe.transpose(ps_rT[b][:, c, :], roped[:, b, c * P:(c + 1) * P], ident)
                mm.then_inc(rT_ready, 1)

            def step(t, b):
                if not known(t, NT - 1):
                    turn_x(t + 1, 1 - b)
                project(t, b)
                if not known(t, 0):
                    turn_r(t - 1, 1 - b)

            turn_x(0, 0)
            tiles(pe, step)
            turn_r(NT - 1, 1)


UNITS1 = [(h, i, k0, n) for h in range(HG) for i in range(TB)
          for k0, n in ([(0, P * (i + 1))] if i < TB // 2 else [(0, HALF), (HALF, P * (i + 1) - HALF)])]
UNITS2 = [(half, j, max(HALF * half, P * j), HALF * (half + 1) - max(HALF * half, P * j), pair)
          for half in range(2) for j in range(4 * half + 4) for pair in range(2)]
N1, N2, NV = len(UNITS1), len(UNITS2), len(UNITS2) // 2
CUTS = [n for n, (half, j, _, _, _) in enumerate(UNITS2) if j >= 4 * half]
LAG = 3
ROWS = 4 * HD + 1
SPREAD = [3, 2] * 9 + [3]
SPREAD += [0] * (N2 - len(SPREAD))
assert sum(SPREAD) == N1


def attention_phase(nc, cst, v_sb, qk_dram):
    ctx = ExitStack()
    with Semaphores(nc) as sems, ctx:
        def sb(name, shape, dt=F32):
            return ctx.enter_context(nc.sbuf_tensor(f"a_{name}", shape, dt))

        def pb(name, shape, dt=F32):
            return ctx.enter_context(nc.psum_tensor(f"a_{name}", shape, dt))

        def sem(name):
            return sems.new(f"a_{name}")

        q_st = [sb(f"q_st{i}", [ROWS, HG, S], F32R) for i in range(3)]
        k_st = [sb(f"k_st{i}", [ROWS, HG, S], F32R) for i in range(3)]
        v_st = [sb(f"v_st{i}", [P, TB, HG, 2 * HD]) for i in range(3)]
        zeros = sb("zeros", [HG * TB, P], F32R)
        probs = sb("probs", [P, 4, 2, HALF])
        unused = sb("unused", [P, 2, HALF], BF16)
        max_a = sb("max_a", [P, HG, TB])
        max_b = sb("max_b", [P, HG, TB // 2])
        max_row = sb("max_row", [HG * TB, P], F32R)
        ctxT = sb("ctxT", [P, 2, HALF])
        recip = sb("recip", [P, 4, HG])
        ps_s = [pb(f"ps_s{i}", [P, 2, HALF]) for i in range(2)]
        ps_m = [pb(f"ps_m{i}", [P, HALF]) for i in range(2)]
        ps_ctx = pb("ps_ctx", [P, HALF])
        ps_turn = pb("ps_turn", [P, 4, P])
        inits, padded = sem("inits"), sem("padded")
        stack_in = [sem(f"stack_in{i}") for i in range(3)]
        max_in = [sem(f"max_in{i}") for i in range(3)]
        v_copied = sem("v_copied")
        scored, exp_done, cut_done, pv_done = sem("scored"), sem("exp_done"), sem("cut_done"), sem("pv_done")
        max_scored, max_read, max_ready, max_turned, max_row_ready = (
            sem("max_scored"), sem("max_read"), sem("max_ready"), sem("max_turned"), sem("max_row_ready"))
        ctx_out, ctx_turned, recip_ready, normalised = sem("ctx_out"), sem("ctx_turned"), sem("recip_ready"), sem("normalised")
        block = ctx.enter_context(nc.Block())
        NGR = B * NG

        def groups(eng, group):
            group(0, 0)
            with eng.Fori(0, (NGR - 4) // 3) as i:
                for r in range(3):
                    group(3 * i + r + 1, (r + 1) % 3)
            for g in range(NGR - 3, NGR):
                group(g, g % 3)

        def is_last(g):
            return isinstance(g, int) and g == NGR - 1

        def is_first(g):
            return isinstance(g, int) and g == 0

        @block.sync
        def _(sp):
            def row_of_max(b):
                return q_st[b][ROWS - 1:ROWS, :, :].rearrange("o h (i s) -> o (h i) s", s=P).bitcast(F32)

            def load(g, b):
                for r in range(4):
                    for qk, stack, part in ((0, q_st[b], r // 2), (1, k_st[b], r % 2)):
                        src = qk_dram[part].rearrange("b g x r s -> (b g) x r s")[bass.ds(g, 1), qk, :, :]
                        sp.dma_start(stack[HD * r:HD * r + HD, :, :].bitcast(F32),
                                     src.rearrange("o (h j) s -> (o j) h s", j=HD)).then_inc(stack_in[b], 16)
                sp.dma_start(row_of_max(b), zeros[:].bitcast(F32)).then_inc(stack_in[b], 16)

            def send_max(g, b):
                sp.wait_ge(max_row_ready, g + 1)
                sp.dma_start(row_of_max(b), max_row[:].bitcast(F32)).then_inc(max_in[b], 16)

            sp.wait_ge(inits, 1)
            load(0, 0)
            load(1, 1)
            send_max(0, 0)

            def group(g, b):
                if not (isinstance(g, int) and g >= NGR - 2):
                    wait(sp, scored, N2 * g)
                    load(g + 2, (b + 2) % 3)
                if not is_last(g):
                    send_max(g + 1, (b + 1) % 3)

            groups(sp, group)

        @block.gpsimd
        def _(pool):
            pool.memset(zeros[:].bitcast(F32), 0.0).then_inc(inits, 1)

            def copy_v(g, b):
                wait(pool, pv_done, NV * (g - 2))
                pool.tensor_copy(v_st[b][:, :, :, 0:HD],
                                 v_sb[:].rearrange("p b g t d -> p (b g) t d")[:, bass.ds(g, 1), :, :]
                                 .rearrange("p o t (h d) -> p (o t) h d", d=HD)).then_inc(v_copied, 1)

            copy_v(0, 0)
            zero = pool.to_reg(0.0)

            def group(g, b):
                for c, n in enumerate(CUTS):
                    pool.wait_ge(exp_done, N2 * g + n + 1)
                    tri = probs[:, n % 4, :, 0:P]
                    alone(pool)
                    pool.affine_select(out=tri, in_=tri, compare_op=ALU.is_ge, fill=zero, base=0, pattern=[[0, 2], [1, P]],
                                       channel_multiplier=-1).then_inc(cut_done, 1)
                    if c == 8 and not is_last(g):
                        copy_v(g + 1, (b + 1) % 3)

            groups(pool, group)

        @block.vector
        def _(dve):
            def read_unit(g, b, r):
                h, i, k0, n = UNITS1[r]
                dve.wait_ge(max_scored, N1 * g + r + 1)
                if not (is_first(g) and r < 2):
                    dve.wait_ge(max_read, N1 * g + r - 1)
                alone(dve)
                ps = ps_m[r % 2][:, 0:n]
                at = max_a[:, h, i:i + 1] if k0 == 0 else max_b[:, h, i - 4:i - 3]
                if k0 + n == P * (i + 1):
                    dve.tensor_tensor_reduce(unused[:, r % 2, 0:n], ps, cst("mask")[:, HALF - n:HALF], 1.0, NEG, ALU.add, ALU.max, at).then_inc(max_read, 1)
                else:
                    dve.tensor_reduce(at, ps, AX.X, ALU.max).then_inc(max_read, 1)

            def join_max(g):
                dve.wait_ge(max_read, N1 * (g + 1))
                wait(dve, max_turned, g)
                late = max_a[:, :, TB // 2:TB]
                dve.tensor_tensor(late, late, max_b[:, :, :], ALU.max).then_inc(max_ready, 1)

            def rows_of_max(g):
                dve.wait_ge(max_turned, g + 1)
                dve.tensor_scalar(max_row[:], ps_turn[0:HG * TB, 0, :], -1.0, None, ALU.mult).then_inc(max_row_ready, 1)

            def divide(g, half, b_prev=None):
                dve.wait_ge(ctx_turned, 2 * g + half + 1)
                sums = ps_turn[:].rearrange("p i (h d) -> p i h d", h=HG)
                dve.reciprocal(recip[:], sums[:, :, :, HD]).then_inc(recip_ready, 1)
                dve.wait_ge(recip_ready, 2 * g + half + 1)
                to = v_sb[:].rearrange("p b g t d -> p (b g) t d")[:, bass.ds(g, 1), 4 * half:4 * half + 4, :]
                to = to.rearrange("p o t (h d) -> p (o t) h d", d=HD)
                dve.tensor_tensor(to, sums[:, :, :, 0:HD], recip[:].unsqueeze(3).to_broadcast([P, 4, HG, HD]), ALU.mult).then_inc(normalised, 1)

            for b in range(3):
                dve.memset(k_st[b][ROWS - 1:ROWS, :, :].bitcast(F32), 1.0)
                dve.memset(v_st[b][:, :, :, HD:HD + 1], 1.0)
                dve.memset(v_st[b][:, :, :, HD + 1:2 * HD], 0.0).then_inc(padded, 1)
            for r in range(N1):
                read_unit(0, 0, r)
            join_max(0)
            rows_of_max(0)

            def group(g, b):
                r = 0
                for s in range(N2):
                    if not is_last(g):
                        for _ in range(SPREAD[s]):
                            read_unit(g + 1, (b + 1) % 3, r)
                            r += 1
                        if s == len([x for x in SPREAD if x]) - 1:
                            join_max(g + 1)
                    if s == LAG + 1 and not is_first(g):
                        divide(g - 1, 1)
                    if s == 12:
                        divide(g, 0)
                    if s == 22 and not is_last(g):
                        rows_of_max(g + 1)

            groups(dve, group)
            divide(NGR - 1, 1)

        @block.scalar
        def _(act):
            def evacuate(g, half):
                act.wait_ge(pv_done, NV * g + 4 + 8 * half)
                wait(act, ctx_turned, 2 * g + half - 1)
                act.activation(ctxT[:, half, :], ps_ctx[:], ACT.Copy).then_inc(ctx_out, 1)

            def group(g, b):
                for s, (half, j, q0, nq, pair) in enumerate(UNITS2):
                    act.wait_ge(scored, N2 * g + s + 1)
                    if not (is_first(g) and s < 4):
                        act.wait_ge(pv_done, NV * g + s // 2 - 1)
                    act.activation(probs[:, s % 4, :, 0:nq], ps_s[s % 2][:, :, 0:nq], ACT.Exp, scale=float(HD) ** -0.5).then_inc(exp_done, 1)
                    if s == 2 and not is_first(g):
                        evacuate(g - 1, 1)
                    if s == 10:
                        evacuate(g, 0)

            groups(act, group)
            evacuate(NGR - 1, 1)

        @block.tensor
        def _(pe):
            ident = cst("ident")

            def first_unit(g, b, r):
                h, i, k0, n = UNITS1[r]
                if not (is_first(g) and r < 2):
                    pe.wait_ge(max_read, N1 * g + r - 1)
                pe.matmul(ps_m[r % 2][:, 0:n], q_st[b][:, h, P * i:P * i + P], k_st[b][:, h, k0:k0 + n],
                          start=True, stop=True).then_inc(max_scored, 1)

            def turn_max(g):
                pe.wait_ge(max_ready, g + 1)
                if not is_first(g):
                    pe.wait_ge(normalised, 2 * g - 1)
                pe.transpose(ps_turn[0:HG * TB, 0, :], max_a[:, :, :].rearrange("p h i -> p (h i)"), ident).then_inc(max_turned, 1)

            def second_unit(g, b, s):
                half, j, q0, nq, pair = UNITS2[s]
                if not (is_first(g) and s < 2):
                    pe.wait_ge(exp_done, N2 * g + s - 1)
                for n in range(2):
                    h = 2 * pair + n
                    mm = pe.matmul(ps_s[s % 2][:, n, 0:nq], k_st[b][:, h, P * j:P * j + P], q_st[b][:, h, q0:q0 + nq],
                                   start=True, stop=True)
                mm.then_inc(scored, 1)

            def times_v(g, b, v):
                half, j, q0, nq, _ = UNITS2[2 * v]
                pe.wait_ge(exp_done, N2 * g + 2 * v + 2)
                if 2 * v in CUTS:
                    pe.wait_ge(cut_done, len(CUTS) * g + CUTS.index(2 * v) + 2)
                if j == 0:
                    wait(pe, ctx_out, 2 * g + half)
                for h in range(HG):
                    mm = pe.matmul(ps_ctx[32 * h:32 * h + 32, q0 - HALF * half:HALF], v_st[b][:, j, h, :],
                                   probs[:, (2 * v + h // 2) % 4, h % 2, 0:nq], start=(j == 0), stop=(j == 4 * half + 3),
                                   skip_group_check=True)
                mm.then_inc(pv_done, 1)

            def turn_ctx(g, half):
                pe.wait_ge(ctx_out, 2 * g + half + 1)
                if half and not is_last(g):
                    pe.wait_ge(max_row_ready, g + 2)
                elif not half and is_first(g):
                    pe.wait_ge(max_row_ready, 1)
                else:
                    pe.wait_ge(normalised, 2 * g + half)
                for i in range(4):
                    mm = pe.transpose(ps_turn[:, i, :], ctxT[:, half, P * i:P * i + P], ident)
                mm.then_inc(ctx_turned, 1)

            pe.wait_ge(padded, 3)
            pe.wait_ge(stack_in[0], 144)
            for r in range(N1):
                first_unit(0, 0, r)
            turn_max(0)

            def group(g, b):
                nxt, prev = (b + 1) % 3, (b + 2) % 3
                r = 0
                for s in range(N2):
                    if s == 0:
                        pe.wait_ge(max_in[b], turns(g, b) * 16)
                        if not is_last(g):
                            pe.wait_ge(stack_in[nxt], turns(g + 1, nxt) * 144)
                    second_unit(g, b, s)
                    if s == 1 and not is_first(g):
                        times_v(g - 1, prev, NV - 1)
                    if not is_last(g):
                        for _ in range(SPREAD[s]):
                            first_unit(g + 1, nxt, r)
                            r += 1
                    if s % 2 == 1 and s >= LAG:
                        if s == LAG:
                            pe.wait_ge(v_copied, g + 1)
                        times_v(g, b, (s - LAG) // 2)
                    if s == LAG + 1 and not is_first(g):
                        turn_ctx(g - 1, 1)
                    if s == 12:
                        turn_ctx(g, 0)
                    if s == 21 and not is_last(g):
                        turn_max(g + 1)

            def turns(g, b):
                if isinstance(g, int):
                    return g // 3 + 1
                return (g - b) // 3 + 1

            groups(pe, group)
            times_v(NGR - 1, (NGR - 1) % 3, NV - 1)
            turn_ctx(NGR - 1, 1)


def output_phase(nc, cst, x_sb, v_sb, wo_hi, wo_lo, x_dram, out):
    ctx = ExitStack()
    with Semaphores(nc) as sems, ctx:
        def sb(name, shape, dt=F32):
            return ctx.enter_context(nc.sbuf_tensor(f"o_{name}", shape, dt))

        def pb(name, shape, dt=F32):
            return ctx.enter_context(nc.psum_tensor(f"o_{name}", shape, dt))

        def sem(name):
            return sems.new(f"o_{name}")

        cx = sb("cx", [P, 2, D])
        cT_hi = sb("cT_hi", [P, 2, KD, P], F32R)
        cT_lo = sb("cT_lo", [P, 2, KD, P], F32R)
        ps_cT = [pb(f"ps_cT{i}", [P, KD, P]) for i in range(2)]
        ps_o = [pb(f"ps_o{i}", [P, D]) for i in range(2)]
        x_in = sem("x_in")
        cx_ready, cT_ready, chi_ready, clo_ready, o_ready, summed = (
            sem("cx_ready"), sem("cT_ready"), sem("chi_ready"), sem("clo_ready"), sem("o_ready"), sem("summed"))
        out_stored = sem("out_stored")
        block = ctx.enter_context(nc.Block())

        def tiles(eng, step):
            step(0, 0)
            step(1, 1)
            with eng.Fori(1, NT // 2) as i:
                for u in range(2):
                    step(2 * i + u, u)

        @block.sync
        def _(sp):
            for q in range(4):
                sp.dma_start(x_sb[:, 8 * q:8 * q + 8, :], x_dram[8 * q * P:8 * (q + 1) * P, :].rearrange("(t p) d -> p t d", p=P)).then_inc(x_in, 16)
            if out is not None:
                sp.wait_ge(summed, NT)
                sp.dma_start(out.rearrange("(t p) d -> p t d", p=P), x_sb[:]).then_inc(out_stored, 16)
                sp.wait_ge(out_stored, 16)

        @block.gpsimd
        def _(pool):
            def step(t, b):
                wait(pool, cT_ready, t - 1)
                pool.tensor_copy(cx[:, b, :].rearrange("p (a g d) -> p a g d", a=1, g=NG),
                                 v_sb[:, bass.ds(t // TB, 1), :, bass.ds(t % TB, 1), :].rearrange("p b g t d -> p (b t) g d")).then_inc(cx_ready, 1)

            tiles(pool, step)

        @block.tensor
        def _(pe):
            def turn(t, b):
                pe.wait_ge(cx_ready, t + 1)
                wait(pe, clo_ready, t - 1)
                for k in range(KD):
                    mm = pe.transpose(ps_cT[b][:, k, :], cx[:, b, k * P:(k + 1) * P], cst("ident"))
                mm.then_inc(cT_ready, 1)

            def product(t, b):
                pe.wait_ge(clo_ready, t + 1)
                wait(pe, summed, t - 1)
                n = 0
                for k in range(KD):
                    for c_part, w_part in ((cT_hi, wo_hi), (cT_hi, wo_lo), (cT_lo, wo_hi)):
                        n += 1
                        mm = pe.matmul(ps_o[b][:], c_part[:, b, k, :], w_part[:, k, :], start=(n == 1), stop=(n == 3 * KD))
                mm.then_inc(o_ready, 1)

            def step(t, b):
                turn(t, b)
                if not (isinstance(t, int) and t == 0):
                    product(t - 1, 1 - b)

            tiles(pe, step)
            product(NT - 1, 1)

        @block.scalar
        def _(act):
            def step(t, b):
                act.wait_ge(cT_ready, t + 1)
                wait(act, o_ready, t - 1)
                act.activation(cT_hi[:, b, :, :], ps_cT[b][:], ACT.Copy).then_inc(chi_ready, 1)

            tiles(act, step)

        @block.vector
        def _(dve):
            def low(t, b):
                dve.wait_ge(chi_ready, t + 1)
                wait(dve, o_ready, t - 1)
                dve.tensor_tensor(cT_lo[:, b, :, :], ps_cT[b][:], cT_hi[:, b, :, :].bitcast(F32), ALU.subtract).then_inc(clo_ready, 1)

            def add(t, b):
                dve.wait_ge(o_ready, t + 1)
                dve.tensor_tensor(x_sb[:, t, :], ps_o[b][:], x_sb[:, t, :], ALU.add).then_inc(summed, 1)

            def step(t, b):
                low(t, b)
                if not (isinstance(t, int) and t == 0):
                    add(t - 1, 1 - b)

            dve.wait_ge(x_in, 64)
            tiles(dve, step)
            add(NT - 1, 1)


def setup_phase(nc, consts, x, gate_w, wq, wk, wv, wo, const_sb, x_sb, gate_sb, qkv_hi, qkv_lo, wo_hi, wo_lo):
    ctx = ExitStack()
    with ctx:
        raw = ctx.enter_context(nc.sbuf_tensor("s_raw", [P, 4, 2, D], F32))
        gate_raw = ctx.enter_context(nc.sbuf_tensor("s_gate_raw", [E, D], F32))
        ps = [ctx.enter_context(nc.psum_tensor(f"s_ps{i}", [P, 2, 2, P], F32)) for i in range(4)]
        ps_gate = ctx.enter_context(nc.psum_tensor("s_ps_gate", [P, KD, E], F32))
        consts_in = ctx.enter_context(nc.semaphore("s_consts_in"))
        w_in = [ctx.enter_context(nc.semaphore(f"s_w_in{i}")) for i in range(5)]
        x_in = ctx.enter_context(nc.semaphore("s_x_in"))
        turned = ctx.enter_context(nc.semaphore("s_turned"))
        hi_done = ctx.enter_context(nc.semaphore("s_hi_done"))
        lo_done = ctx.enter_context(nc.semaphore("s_lo_done"))
        block = ctx.enter_context(nc.Block())

        def cst(name):
            at, w = CONST_AT[name]
            return const_sb[:, at:at + w]

        def parts(m):
            if m == 3:
                return wo_hi[:], wo_lo[:]
            return qkv_hi[:, :, m * D:(m + 1) * D], qkv_lo[:, :, m * D:(m + 1) * D]

        @block.sync
        def _(sp):
            sp.dma_start(const_sb[:], consts).then_inc(consts_in, 16)
            sp.dma_start(gate_raw[:], gate_w).then_inc(w_in[4], 16)
            for m, w in enumerate((wq, wk, wv, wo)):
                sp.dma_start(raw[:, m, :, :], w.rearrange("(c p) h -> p c h", p=P)).then_inc(w_in[m], 16)
            sp.wait_ge(x_in, 64)

        @block.scalar
        def _(act):
            for q in range(4):
                act.dma_start(x_sb[:, 8 * q:8 * q + 8, :], x[8 * q * P:8 * (q + 1) * P, :].rearrange("(t p) d -> p t d", p=P)).then_inc(x_in, 16)
            for m in range(4):
                act.wait_ge(turned, m + 2)
                act.activation(parts(m)[0].rearrange("p k (c o) -> p k c o", c=2), ps[m][:], ACT.Copy).then_inc(hi_done, 1)

        @block.tensor
        def _(pe):
            pe.wait_ge(consts_in, 16)
            pe.wait_ge(w_in[4], 16)
            for k in range(KD):
                mm = pe.transpose(ps_gate[:, k, :], gate_raw[:, k * P:(k + 1) * P], cst("ident")[0:E, 0:E])
            mm.then_inc(turned, 1)
            for m in range(4):
                pe.wait_ge(w_in[m], 16)
                for k in range(KD):
                    for c in range(2):
                        mm = pe.transpose(ps[m][:, k, c, :], raw[:, m, c, k * P:(k + 1) * P], cst("ident"))
                mm.then_inc(turned, 1)

        @block.vector
        def _(dve):
            dve.wait_ge(turned, 1)
            dve.tensor_copy(gate_sb[:], ps_gate[:])
            for m in range(4):
                dve.wait_ge(hi_done, m + 1)
                hi, lo = parts(m)
                dve.tensor_tensor(lo.rearrange("p k (c o) -> p k c o", c=2), ps[m][:],
                                  hi.bitcast(F32).rearrange("p k (c o) -> p k c o", c=2), ALU.subtract).then_inc(lo_done, 1)


def program(nc, consts, x, gate_w, w_gate, w_up, w_down, wq, wk, wv, wo, out, phases=("ffn1", "attn", "ffn2")):
    ctx = ExitStack()
    with ctx:
        def sb(name, shape, dt=F32):
            return ctx.enter_context(nc.sbuf_tensor(name, shape, dt))

        x = x.rearrange("b s d -> (b s) d")
        out = out.rearrange("b s d -> (b s) d")
        const_sb = sb("const_sb", [P, CONST_N])
        gate_sb = sb("gate_sb", [P, KD, E])
        qkv_hi, qkv_lo = (sb(f"qkv_{p}", [P, KD, 3 * D], F32R) for p in ("hi", "lo"))
        wo_hi, wo_lo = (sb(f"wo_{p}", [P, KD, D], F32R) for p in ("hi", "lo"))
        xn_dram = nc.dram_tensor("xn_dram", [T, D], F32, kind="Internal").ap()
        y_dram = nc.dram_tensor("y_dram", [T * TOPK, D], F32, kind="Internal").ap()
        x_dram = nc.dram_tensor("x_dram", [T, D], F32, kind="Internal").ap()
        qk_dram = nc.dram_tensor("qk_dram", [2, B, NG, 2, HG * HD, S], F32, kind="Internal").ap()

        def cst(name):
            at, w = CONST_AT[name]
            return const_sb[:, at:at + w]

        v_sb = sb("v_sb", [P, B, NG, TB, HG * HD])
        spare = v_sb[:].rearrange("p b g t d -> p (b g t d)")
        with nc.sbuf_tensor("x_before", [P, NT, D], F32) as x_sb:
            setup_phase(nc, consts, x, gate_w, wq, wk, wv, wo, const_sb, x_sb, gate_sb, qkv_hi, qkv_lo, wo_hi, wo_lo)
            if "ffn1" in phases:
                ffn_phase(nc, "f1", cst, x_sb, gate_sb, w_gate, w_up, w_down, xn_dram, y_dram, spare, out if phases[-1] == "ffn1" else x_dram)
                if phases[-1] == "ffn1":
                    return
            projection_phase(nc, cst, x_sb, v_sb, qkv_hi, qkv_lo, qk_dram)
        attention_phase(nc, cst, v_sb, qk_dram)
        with nc.sbuf_tensor("x_after", [P, NT, D], F32) as x_sb:
            output_phase(nc, cst, x_sb, v_sb, wo_hi, wo_lo, x_dram if "ffn1" in phases else x, out if phases[-1] == "attn" else None)
            if "ffn2" in phases:
                ffn_phase(nc, "f2", cst, x_sb, gate_sb, w_gate, w_up, w_down, xn_dram, y_dram, spare, out)


INPUTS = ["L0_attn_hidden_states", "L0_ffn_gate_w", "L0_ffn_w_gate", "L0_ffn_w_up", "L0_ffn_w_down",
          "L0_attn_Wq", "L0_attn_Wk", "L0_attn_Wv", "L0_attn_Wo"]


def kernel(**inputs):
    import concourse.bacc as bacc
    from concourse.bass_utils import run_bass_kernel_spmd

    nc = bacc.Bacc("TRN2", target_bir_lowering=False, num_devices=1)
    arrays = {"consts": constants()}
    arrays.update({name: np.ascontiguousarray(inputs[name]) for name in INPUTS})
    args = [nc.dram_tensor(name, a.shape, mybir.dt.from_np(a.dtype), kind="ExternalInput").ap() for name, a in arrays.items()]
    out = nc.dram_tensor("out", (B, S, D), F32, kind="ExternalOutput").ap()
    program(nc, *args, out)
    return run_bass_kernel_spmd(nc, [arrays], core_ids=[0]).results[0]["out"]
```

```python
from contextlib import ExitStack

import numpy as np
import concourse.bass as bass
from concourse import mybir
from concourse.alu_op_type import AluOpType as ALU

F32 = mybir.dt.float32
F32R = mybir.dt.float32r
BF16 = mybir.dt.bfloat16
I32 = mybir.dt.int32
U32 = mybir.dt.uint32
ACT = mybir.ActivationFunctionType
AX = mybir.AxisListType

P = 128
B, S, D = 4, 1024, 256
T = B * S
NT = T // P
TB = S // P
KD = D // P
E, F, TOPK = 8, 176, 2
FH = F // 2
SLOT_TILES = TOPK * NT + E - 1
EPS = 1e-5
NH, HD = 16, 16
HG = 4
NG = NH // HG
HALF = 512
NEG = -3.0e38
EMPTY = 1.0e6

CONST_WIDTHS = [("ident", 128), ("before", 128), ("mask", 512), ("cos", NT * HD), ("sin", NT * HD),
                ("expert", E * NT), ("full", E * NT), ("count", 128), ("pair1", TOPK * NT)]
CONST_AT = {}
for _name, _w in CONST_WIDTHS:
    CONST_AT[_name] = (sum(w for _, w in CONST_WIDTHS[:len(CONST_AT)]), _w)
CONST_N = sum(w for _, w in CONST_WIDTHS)


def constants():
    c = np.zeros((P, CONST_N), np.float32)

    def put(name, value):
        at, w = CONST_AT[name]
        c[:, at:at + w] = np.broadcast_to(np.asarray(value, np.float32).reshape(-1, w), (P, w))

    p = np.arange(P)
    put("ident", np.eye(P))
    put("before", (p[:, None] < p[None, :]))
    mask = np.zeros((P, 512), np.float32)
    mask[:, 384:] = np.where(p[None, :] <= p[:, None], 0.0, NEG)
    put("mask", mask)
    inv_freq = (np.float32(1.0) / np.float32(10000.0) ** (np.arange(0, HD, 2, dtype=np.float32) / np.float32(HD))).astype(np.float32)
    pos = (np.arange(NT)[None, :] % TB * P + p[:, None]).astype(np.float32)
    angle = (pos[:, :, None] * inv_freq).astype(np.float32)
    cos, sin = np.cos(angle), np.sin(angle)
    put("cos", np.concatenate([cos, cos], axis=2).reshape(P, -1))
    put("sin", np.concatenate([-sin, sin], axis=2).reshape(P, -1))
    put("expert", np.repeat(np.arange(E), NT))
    put("full", np.tile(np.arange(NT) * P, E))
    put("count", np.arange(128))
    put("pair1", TOPK * (P * np.arange(NT)[None, None, :] + p[:, None, None]) + np.arange(TOPK)[None, :, None] + 1)
    return c


def alone(eng):
    eng.nop(nofuse=True)


class Own:

    def __init__(self, eng, sem):
        self.eng, self.sem, self.n = eng, sem, 0

    def inc(self, ins):
        ins.then_inc(self.sem, 1)
        self.n = self.n + 1

    def wait(self):
        self.eng.wait_ge(self.sem, self.n)

    def then_wait(self, ins):
        self.inc(ins)
        self.wait()


class Semaphores:

    def __init__(self, nc):
        self.nc, self.taken = nc, []

    def __enter__(self):
        return self

    def new(self, name):
        self.taken.append(self.nc.alloc_semaphore(name=name))
        return self.taken[-1]

    def __exit__(self, *_):
        self.nc.clear_and_free_semaphores(self.taken)
        self.nc.all_engine_barrier()


def ffn_phase(nc, tag, cst, x_sb, gate_sb, w_gate, w_up, w_down, xn_dram, y_dram, spare, out):
    ctx = ExitStack()
    with Semaphores(nc) as sems, ctx:
        def sb(name, shape, dt=F32):
            return ctx.enter_context(nc.sbuf_tensor(f"{tag}_{name}", shape, dt))

        def pb(name, shape, dt=F32):
            return ctx.enter_context(nc.psum_tensor(f"{tag}_{name}", shape, dt))

        def sem(name):
            return sems.new(f"{tag}_{name}")

        carved = [0]

        def carve(rows, *shape):
            n = int(np.prod(shape))
            at, carved[0] = carved[0], carved[0] + n
            names = "abcd"[:len(shape)]
            return spare[0:rows, at:at + n].rearrange(f"p ({' '.join(names)}) -> p {' '.join(names)}", **dict(zip(names, shape)))

        gu_hi = sb("gu_hi", [P, E, KD, 2 * F], F32R)
        gu_lo = sb("gu_lo", [P, E, KD, 2 * F], F32R)
        dn_hi = sb("dn_hi", [FH, E, 2, D], F32R)
        dn_lo = sb("dn_lo", [FH, E, 2, D], F32R)
        gu_raw = carve(P, 2, KD, 2 * F)
        dn_raw = carve(FH, 2, 2, D)
        stats = sb("stats", [P, 8, 6])
        mv = sb("mv", [P, 8, 2])
        rstd = sb("rstd", [P, NT])
        nmr = sb("nmr", [P, NT])
        minus_half = sb("minus_half", [P, 8])
        xn = sb("xn", [P, 4, D])
        xnT = sb("xnT", [P, 2, KD, P])
        best = sb("best", [P, 4, 8])
        best_at = sb("best_at", [P, 4, 8], U32)
        gap = sb("gap", [P, NT])
        egap = sb("egap", [P, NT])
        den = sb("den", [P, NT])
        w_mix = sb("w_mix", [P, TOPK, NT])
        choice = sb("choice", [P, TOPK, NT])
        hot = sb("hot", [P, TOPK, E, NT])
        hot_sum = sb("hot_sum", [P, E * NT], BF16)
        before_bf = sb("before_bf", [P, P], BF16)
        ones_bf = sb("ones_bf", [P, P], BF16)
        totals = sb("totals", [P, E, NT])
        running = sb("running", [P, E, NT])
        base = sb("base", [P, E, NT])
        work = sb("work", [P, SLOT_TILES * E])
        n_tiles = sb("n_tiles", [P, E])
        last_tile = sb("last_tile", [P, E])
        first_tile = sb("first_tile", [P, E])
        expert_f = sb("expert_f", [P, SLOT_TILES])
        expert_of = sb("expert_of", [P, SLOT_TILES], I32)
        slot_f = sb("slot_f", [P, TOPK * NT])
        slot_i = sb("slot_i", [P, TOPK * NT], I32)
        slot_ji = sb("slot_ji", [P, TOPK * NT], I32)
        slot_pi = sb("slot_pi", [P, TOPK * NT], I32)
        slot_j = sb("slot_j", [P, TOPK * NT])
        slot_p = sb("slot_p", [P, TOPK * NT])
        zero_bf = sb("zero_bf", [P, SLOT_TILES], BF16)
        at_row = sb("at_row", [P, 4, P])
        at_tile = sb("at_tile", [P, 4, SLOT_TILES])
        owner = sb("owner", [P, SLOT_TILES])
        empty = sb("empty", [P, SLOT_TILES])
        pair_i = sb("pair_i", [P, SLOT_TILES], I32)
        token_i = sb("token_i", [P, SLOT_TILES], I32)
        token_now = sb("token_now", [P, 2, 4], I32)
        pair_now = sb("pair_now", [P, 2, 4], I32)
        xg = carve(P, 4, D)
        xT_hi = sb("xT_hi", [P, 2, KD, P], F32R)
        xT_lo = sb("xT_lo", [P, 2, KD, P], F32R)
        sg = sb("sg", [P, 2, F])
        h = sb("h", [P, 2, F])
        hT_hi = sb("hT_hi", [FH, 2, 2, P], F32R)
        hT_lo = sb("hT_lo", [FH, 2, 2, P], F32R)
        y_sb = carve(P, 4, D)
        carved[0] = 0
        yb = carve(P, 8, TOPK, D)

        ps_xT = [pb(f"ps_xT{i}", [P, KD, P]) for i in range(2)]
        ps_gu = [pb(f"ps_gu{i}", [P, 2 * F]) for i in range(2)]
        ps_hT = [pb(f"ps_hT{i}", [FH, 2, P]) for i in range(2)]
        ps_y = [pb(f"ps_y{i}", [P, D]) for i in range(2)]
        ps_lg = [bank[:, 0:E] for bank in (ps_gu[0], ps_gu[1], ps_y[0], ps_y[1])]
        ps_before = ps_gu[1][:, 0:E * NT].rearrange("p (e t) -> p e t", e=E)
        ps_total = ps_y[0][:, 0:E * NT].rearrange("p (e t) -> p e t", e=E)
        ps_owner = ps_y[1][:, 0:SLOT_TILES]

        gu_in = [sem(f"gu_in{i}") for i in range(2)]
        dn_in = [sem(f"dn_in{i}") for i in range(2)]
        w_parts, w_own = sem("w_parts"), sem("w_own")
        stats_own, moments = sem("stats_own"), sem("moments")
        variances = sem("variances")
        xn_ready, xn_turned, xnT_ready, logits_done = sem("xn_ready"), sem("xn_turned"), sem("xnT_ready"), sem("logits_done")
        xn_stored = [sem(f"xn_stored{i}") for i in range(4)]
        dve_own, gap_ready, egap_ready = sem("dve_own"), sem("gap_ready"), sem("egap_ready")
        best_ready, index_ready = sem("best_ready"), sem("index_ready")
        hot_ready, ranks_ready = sem("hot_ready"), sem("ranks_ready")
        one_hot_ready, one_hot_used = sem("one_hot_ready"), sem("one_hot_used")
        owner_ready, slots_ready, pool_init = sem("owner_ready"), sem("slots_ready"), sem("pool_init")
        now_ready = sem("now_ready")
        gathered = [sem(f"gathered{i}") for i in range(4)]
        scattered = [sem(f"scattered{i}") for i in range(4)]
        xT_ready, xhi_ready, xlo_ready = sem("xT_ready"), sem("xhi_ready"), sem("xlo_ready")
        gu_ready, sg_ready, h_ready = sem("gu_ready"), sem("sg_ready"), sem("h_ready")
        hT_ready, hhi_ready, hlo_ready = sem("hT_ready"), sem("hhi_ready"), sem("hlo_ready")
        y_ready, y_out = sem("y_ready"), sem("y_out")
        y_in = [sem(f"y_in{i}") for i in range(8)]
        mixed, mix_own = sem("mixed"), sem("mix_own")
        out_stored = sem("out_stored")

        block = ctx.enter_context(nc.Block())

        def gu_src(w, e):
            return w[e, :, :].rearrange("(k p) f -> p k f", p=P)

        def expert_steps(eng, step):
            for j in range(8):
                step(j, j % 4)
            with eng.Fori(2, SLOT_TILES // 4 - 1) as i:
                for u in range(4):
                    step(4 * i + u, u)
            for j in range(4 * (SLOT_TILES // 4 - 1), SLOT_TILES + 2):
                step(j, j % 4)

        def is_tile(j):
            return not isinstance(j, int) or 0 <= j < SLOT_TILES

        @block.sync
        def _(sp):
            for e in range(E):
                if e >= 2:
                    sp.wait_ge(w_parts, 2 * (e - 1))
                sp.dma_start(gu_raw[:, e % 2, :, 0:F], gu_src(w_gate, e)).then_inc(gu_in[e % 2], 16)
                sp.dma_start(gu_raw[:, e % 2, :, F:2 * F], gu_src(w_up, e)).then_inc(gu_in[e % 2], 16)
                sp.dma_start(dn_raw[:, e % 2, :, :], w_down[e, :, :].rearrange("(c p) d -> p c d", p=FH)).then_inc(dn_in[e % 2], 16)
                for t in range(4 * e, 4 * e + 4):
                    sp.wait_ge(xn_ready, t + 1)
                    sp.dma_start(xn_dram[t * P:(t + 1) * P, :], xn[:, t % 4, :]).then_inc(xn_stored[t % 4], 16)
            for q in range(4):
                sp.wait_ge(scattered[q], 16 * len(range(q, SLOT_TILES, 4)))
            with sp.Fori(0, NT // 8) as i:
                for u in range(8):
                    t = 8 * i + u
                    sp.wait_ge(mixed, t - 7 + 8)
                    sp.dma_start(yb[:, u, :, :].rearrange("p c d -> p (c d)"),
                                 y_dram[bass.ds(t * P * TOPK, P * TOPK), :].rearrange("(p c) d -> p (c d)", c=TOPK)
                                 ).then_inc(y_in[u], 16)
            if out is not None:
                for q in range(4):
                    sp.wait_ge(mixed, 8 + 8 * (q + 1))
                    sp.dma_start(out[q * 8 * P:(q + 1) * 8 * P, :].rearrange("(t p) d -> p t d", p=P),
                                 x_sb[:, 8 * q:8 * q + 8, :]).then_inc(out_stored, 16)
                sp.wait_ge(out_stored, 64)

        @block.gpsimd
        def _(pool):
            own = Own(pool, w_own)
            own.then_wait(pool.memset(minus_half[:], -0.5))
            for e in range(E):
                if e % 2 == 0:
                    q = slice(4 * e, 4 * e + 8)
                    pool.wait_ge(variances, e // 2 + 1)
                    own.then_wait(pool.tensor_tensor(rstd[:, q], rstd[:, q], minus_half[:], ALU.pow))
                    pool.tensor_tensor(nmr[:, q], nmr[:, q], rstd[:, q], ALU.mult).then_inc(moments, 1)
                pool.wait_ge(gu_in[e % 2], 32 * (e // 2 + 1))
                own.then_wait(pool.tensor_copy(gu_hi[:, e, :, :], gu_raw[:, e % 2, :, :]))
                pool.tensor_tensor(gu_lo[:, e, :, :], gu_raw[:, e % 2, :, :], gu_hi[:, e, :, :].bitcast(F32),
                                   ALU.subtract).then_inc(w_parts, 1)
                pool.wait_ge(dn_in[e % 2], 16 * (e // 2 + 1))
                own.then_wait(pool.tensor_copy(dn_hi[:, e, :, :], dn_raw[:, e % 2, :, :]))
                pool.tensor_tensor(dn_lo[:, e, :, :], dn_raw[:, e % 2, :, :], dn_hi[:, e, :, :].bitcast(F32),
                                   ALU.subtract).then_inc(w_parts, 1)
            pool.memset(xg, 0.0).then_inc(pool_init, 1)
            pool.wait_ge(pool_init, 1)
            for q in range(4):
                pool.wait_ge(xn_stored[q], 16 * (NT // 4))
            pool.wait_ge(slots_ready, 1)

            last_token, last_pair = pool.to_reg(T - 1), pool.to_reg(TOPK * T - 1)

            def gather(slot, token):
                alone(pool)
                pool.indirect_dma_start(xg[:, slot, :], None, xn_dram, bass.IndirectOffsetOnAxis(ap=token, axis=0),
                                        bounds_check=last_token, oob_is_err=False).then_inc(gathered[slot], 16)

            def scatter(j, slot, pair):
                pool.wait_ge(y_out, j + 1)
                alone(pool)
                pool.indirect_dma_start(y_dram, bass.IndirectOffsetOnAxis(ap=pair, axis=0), y_sb[:, slot, :], None,
                                        bounds_check=last_pair, oob_is_err=False).then_inc(scattered[slot], 16)

            def step(j, u, token, pair):
                if token is not None:
                    wait(pool, xT_ready, j + 2)
                    gather((u + 5) % 4, token)
                if pair is not None:
                    scatter(j - 2, (u - 2) % 4, pair)

            def fixed_step(j):
                step(j, j % 4, token_i[:, j + 5:j + 6] if is_tile(j + 5) else None, pair_i[:, j - 2:j - 1] if is_tile(j - 2) else None)

            LOOPED = 2 * ((SLOT_TILES - 5) // 8 - 1)
            for j in range(-5, 4):
                fixed_step(j)
            with pool.Fori(0, LOOPED // 2) as i:
                for r in range(2):
                    turn = 2 * i + r + 1
                    pool.tensor_copy(token_now[:, r, :], token_i[:, bass.ds(4 * turn + 5, 4)]).then_inc(now_ready, 1)
                    pool.tensor_copy(pair_now[:, r, :], pair_i[:, bass.ds(4 * turn - 2, 4)]).then_inc(now_ready, 1)
                    pool.wait_ge(now_ready, 2 * turn)
                    for u in range(4):
                        step(4 * turn + u, u, token_now[:, r, u:u + 1], pair_now[:, r, u:u + 1])
            for j in range(4 * LOOPED + 4, SLOT_TILES + 2):
                fixed_step(j)

        @block.vector
        def _(dve):
            own = Own(dve, stats_own)
            dve.sem_inc(mixed, 8)
            with dve.Fori(0, NT // 8) as i:
                own.n = i * 16
                for u in range(8):
                    own.inc(dve.bn_stats(stats[:, u, :], x_sb[:, 8 * i + u, :]))
                own.wait()
                alone(dve)
                for u in range(8):
                    own.inc(dve.bn_aggr(mv[:, u, :], stats[:, u, :]))
                own.wait()
                dve.tensor_scalar(rstd[:, bass.ds(8 * i, 8)], mv[:, :, 1], EPS, None, ALU.add)
                dve.tensor_scalar(nmr[:, bass.ds(8 * i, 8)], mv[:, :, 0], -1.0, None, ALU.mult).then_inc(variances, 1)
            own = Own(dve, dve_own)
            def take_max(t, u):
                dve.wait_ge(logits_done, t + 1)
                alone(dve)
                dve.max(best[:, u, :], ps_lg[u]).then_inc(best_ready, 1)

            def take_index(t, u):
                dve.wait_ge(best_ready, t + 1)
                alone(dve)
                dve.max_index(best_at[:, u, :], best[:, u, :], ps_lg[u]).then_inc(index_ready, 1)
                dve.tensor_tensor(gap[:, bass.ds(t, 1)], best[:, u, 1:2], best[:, u, 0:1], ALU.subtract)

            def keep_index(t, u, last=False):
                dve.wait_ge(index_ready, t + 1)
                ins = dve.tensor_copy(choice[:, :, bass.ds(t, 1)].rearrange("p c a -> p (c a)"), best_at[:, u, 0:TOPK])
                if last:
                    ins.then_inc(gap_ready, 1)

            for t in range(4):
                take_max(t, t)
                if t >= 1:
                    take_index(t - 1, t - 1)
                if t >= 2:
                    keep_index(t - 2, t - 2)
            with dve.Fori(1, NT // 4) as i:
                for u in range(4):
                    take_max(4 * i + u, u)
                    take_index(4 * i + u - 1, (u + 3) % 4)
                    keep_index(4 * i + u - 2, (u + 2) % 4)
            take_index(NT - 1, 3)
            keep_index(NT - 2, 2)
            keep_index(NT - 1, 3, True)
            dve.wait_ge(gap_ready, 1)
            own.inc(dve.tensor_copy(before_bf[:], cst("before")))
            own.inc(dve.memset(ones_bf[:], 1.0))
            own.then_wait(dve.memset(zero_bf[:], 0.0))
            expert_c = cst("expert").rearrange("p (e t) -> p e t", e=E)
            for c in range(TOPK):
                own.inc(dve.tensor_tensor(hot[:, c, :, :], choice[:, c, :].unsqueeze(1).to_broadcast([P, E, NT]), expert_c, ALU.is_equal))
            own.wait()
            dve.tensor_tensor(hot_sum[:].rearrange("p (e t) -> p e t", e=E), hot[:, 0, :, :], hot[:, 1, :, :], ALU.add).then_inc(hot_ready, 1)
            dve.wait_ge(egap_ready, 1)
            own.then_wait(dve.tensor_scalar(den[:], egap[:], 1.0, None, ALU.add))
            own.then_wait(dve.reciprocal(gap[:], den[:]))
            own.inc(dve.tensor_scalar(w_mix[:, 0, :], gap[:], 0.5, None, ALU.mult))
            own.inc(dve.scalar_tensor_tensor(w_mix[:, 1, :], egap[:], 0.5, gap[:], ALU.mult, ALU.mult))
            dve.wait_ge(ranks_ready, 1)
            own.then_wait(dve.tensor_copy(totals[:], ps_total))
            ones_t = ones_bf[:, 0:NT]
            for e in range(E):
                own.inc(dve.tensor_tensor_scan(running[:, e, :], ones_t, totals[:, e, :], 0.0, ALU.mult, ALU.add))
            own.wait()
            full = cst("full").rearrange("p (e t) -> p e t", e=E)
            begun = work[:, 0:E * NT].rearrange("p (e t) -> p e t", e=E)
            own.then_wait(dve.tensor_tensor(begun, running[:, :, NT - 1:NT].to_broadcast([P, E, NT]), full, ALU.is_gt))
            own.then_wait(dve.tensor_reduce(n_tiles[:], begun, AX.X, ALU.add))
            own.then_wait(dve.tensor_tensor_scan(last_tile[:], ones_bf[:, 0:E], n_tiles[:], 0.0, ALU.mult, ALU.add))
            own.inc(dve.tensor_tensor(first_tile[:], last_tile[:], n_tiles[:], ALU.subtract))
            own.then_wait(dve.tensor_tensor(running[:], running[:], totals[:], ALU.subtract))
            own.then_wait(dve.tensor_tensor(totals[:], ps_before, running[:], ALU.add))
            own.then_wait(dve.scalar_tensor_tensor(base[:], first_tile[:].unsqueeze(2).to_broadcast([P, E, NT]), float(P), totals[:],
                                                   ALU.mult, ALU.add))
            for c in range(TOPK):
                own.then_wait(dve.tensor_tensor(hot[:, c, :, :], hot[:, c, :, :], base[:], ALU.mult))
                own.inc(dve.tensor_reduce(slot_f[:, c * NT:(c + 1) * NT], hot[:, c, :, :].rearrange("p e t -> p t e"), AX.X, ALU.add))
            own.wait()
            own.then_wait(dve.tensor_copy(slot_i[:], slot_f[:]))
            own.inc(dve.tensor_scalar(slot_ji[:], slot_i[:], 7, None, ALU.logical_shift_right))
            own.then_wait(dve.tensor_scalar(slot_pi[:], slot_i[:], P - 1, None, ALU.bitwise_and))
            own.inc(dve.tensor_copy(slot_j[:], slot_ji[:]))
            own.then_wait(dve.tensor_copy(slot_p[:], slot_pi[:]))
            begun_j = work[:].rearrange("p (j e) -> p j e", e=E)
            own.then_wait(dve.tensor_tensor(begun_j, cst("count")[:, 0:SLOT_TILES].unsqueeze(2).to_broadcast([P, SLOT_TILES, E]),
                                            first_tile[:].unsqueeze(1).to_broadcast([P, SLOT_TILES, E]), ALU.is_ge))
            own.then_wait(dve.tensor_reduce(expert_f[:], begun_j, AX.X, ALU.add))
            own.inc(dve.tensor_scalar(expert_of[:], expert_f[:], -1.0, None, ALU.add))
            with dve.Fori(0, TOPK * NT // 4) as i:
                for u in range(4):
                    at = 4 * i + u
                    dve.wait_ge(one_hot_used, at + 1)
                    dve.tensor_scalar(at_row[:, u, :], cst("count"), slot_p[:, bass.ds(at, 1)], None, ALU.is_equal)
                    dve.tensor_scalar(at_tile[:, u, :], cst("count")[:, 0:SLOT_TILES], slot_j[:, bass.ds(at, 1)],
                                      cst("pair1")[:, bass.ds(at, 1)], ALU.is_equal, ALU.mult).then_inc(one_hot_ready, 1)
            dve.wait_ge(owner_ready, 1)
            own.then_wait(dve.tensor_copy(owner[:], ps_owner))
            own.then_wait(dve.tensor_scalar(empty[:], owner[:], 0.0, EMPTY, ALU.is_equal, ALU.mult))
            own.then_wait(dve.scalar_tensor_tensor(pair_i[:], owner[:], -1.0, empty[:], ALU.add, ALU.add))
            dve.tensor_scalar(token_i[:], pair_i[:], 1, None, ALU.logical_shift_right).then_inc(slots_ready, 1)

            def x_low(j, b):
                dve.wait_ge(xhi_ready, j + 1)
                wait(dve, gu_ready, j - 1)
                dve.tensor_tensor(xT_lo[:, b, :, :], ps_xT[b][:], xT_hi[:, b, :, :].bitcast(F32), ALU.subtract).then_inc(xlo_ready, 1)

            def h_product(j, b):
                dve.wait_ge(sg_ready, j + 1)
                wait(dve, hT_ready, j - 1)
                dve.tensor_tensor(h[:, b, :], ps_gu[b][:, F:2 * F], sg[:, b, :], ALU.mult).then_inc(h_ready, 1)

            def h_low(j, b):
                dve.wait_ge(hhi_ready, j + 1)
                wait(dve, y_ready, j - 1)
                dve.tensor_tensor(hT_lo[:, b, :, :], ps_hT[b][:], hT_hi[:, b, :, :].bitcast(F32), ALU.subtract).then_inc(hlo_ready, 1)

            def steps(j, u):
                b = u % 2
                if is_tile(j):
                    h_product(j, b)
                if is_tile(j - 1):
                    h_low(j - 1, 1 - b)
                if is_tile(j + 2):
                    x_low(j + 2, b)

            x_low(0, 0)
            x_low(1, 1)
            expert_steps(dve, steps)

            def mix(t, u, c):
                dve.scalar_tensor_tensor(x_sb[:, t, :], yb[:, u, c, :], w_mix[:, c, bass.ds(t, 1)], x_sb[:, t, :],
                                         ALU.mult, ALU.add).then_inc(mixed if c else mix_own, 1)

            def mix_step(t, u):
                dve.wait_ge(y_in[u], 2 * (t - u) + 16)
                mix(t, u, 0)
                if not known(t, 0):
                    dve.wait_ge(mix_own, t)
                    mix(t - 1, (u - 1) % 8, 1)

            for t in range(8):
                mix_step(t, t)
            with dve.Fori(1, NT // 8) as i:
                for u in range(8):
                    mix_step(8 * i + u, u)
            dve.wait_ge(mix_own, NT)
            mix(NT - 1, 7, 1)

        @block.scalar
        def _(act):
            def normalise(t, u):
                act.wait_ge(moments, (t // 8) + 1)
                wait(act, xn_stored[u], (t - u) * 4)
                wait(act, xn_turned, t - 3)
                act.activation(xn[:, u, :], x_sb[:, t, :], ACT.Identity, bias=nmr[:, bass.ds(t, 1)], scale=rstd[:, bass.ds(t, 1)]).then_inc(xn_ready, 1)

            def turn_copy(t, b):
                act.wait_ge(xn_turned, t + 1)
                wait(act, logits_done, t - 1)
                act.activation(xnT[:, b, :, :], ps_xT[b][:], ACT.Copy).then_inc(xnT_ready, 1)

            for t in range(8):
                normalise(t, t % 4)
                if t:
                    turn_copy(t - 1, (t - 1) % 2)
            with act.Fori(2, NT // 4) as i:
                for u in range(4):
                    normalise(4 * i + u, u)
                    turn_copy(4 * i + u - 1, (u + 1) % 2)
            turn_copy(NT - 1, 1)
            act.wait_ge(gap_ready, 1)
            act.activation(egap[:], gap[:], ACT.Exp).then_inc(egap_ready, 1)

            def x_high(j, b):
                act.wait_ge(xT_ready, j + 1)
                wait(act, gu_ready, j - 1)
                act.activation(xT_hi[:, b, :, :], ps_xT[b][:], ACT.Copy).then_inc(xhi_ready, 1)

            def y_copy(j, u):
                act.wait_ge(y_ready, j + 1)
                wait(act, scattered[u], (j - u) * 4)
                act.activation(y_sb[:, u, :], ps_y[u % 2][:], ACT.Copy).then_inc(y_out, 1)

            def silu(j, b):
                act.wait_ge(gu_ready, j + 1)
                wait(act, h_ready, j - 1)
                act.activation(sg[:, b, :], ps_gu[b][:, 0:F], ACT.Silu).then_inc(sg_ready, 1)

            def h_high(j, b):
                act.wait_ge(hT_ready, j + 1)
                wait(act, y_ready, j - 1)
                act.activation(hT_hi[:, b, :, :], ps_hT[b][:], ACT.Copy).then_inc(hhi_ready, 1)

            def steps(j, u):
                b = u % 2
                if is_tile(j):
                    silu(j, b)
                if is_tile(j - 1):
                    h_high(j - 1, 1 - b)
                if is_tile(j + 2):
                    x_high(j + 2, b)
                if is_tile(j - 2):
                    y_copy(j - 2, (u + 2) % 4)

            x_high(0, 0)
            x_high(1, 1)
            expert_steps(act, steps)

        @block.tensor
        def _(pe):
            ident = cst("ident")
            def turn(t, u):
                b = u % 2
                pe.wait_ge(xn_ready, t + 1)
                wait(pe, xnT_ready, t - 1)
                for k in range(KD):
                    mm = pe.transpose(ps_xT[b][:, k, :], xn[:, u, k * P:(k + 1) * P], ident)
                mm.then_inc(xn_turned, 1)

            def logits(t, u):
                b = u % 2
                pe.wait_ge(xnT_ready, t + 1)
                wait(pe, index_ready, t - 3)
                for k in range(KD):
                    mm = pe.matmul(ps_lg[u], xnT[:, b, k, :], gate_sb[:, k, :], start=(k == 0), stop=(k == KD - 1))
                mm.then_inc(logits_done, 1)

            for t in range(8):
                turn(t, t % 4)
                if t:
                    logits(t - 1, (t - 1) % 4)
            with pe.Fori(2, NT // 4) as i:
                for u in range(4):
                    turn(4 * i + u, u)
                    logits(4 * i + u - 1, (u + 3) % 4)
            logits(NT - 1, 3)
            pe.wait_ge(hot_ready, 1)
            pe.matmul(ps_before.rearrange("p e t -> p (e t)"), before_bf[:], hot_sum[:], start=True, stop=True)
            pe.matmul(ps_total.rearrange("p e t -> p (e t)"), ones_bf[:], hot_sum[:], start=True, stop=True).then_inc(ranks_ready, 1)
            pe.matmul(ps_owner, before_bf[:], zero_bf[:], start=True, stop=False)
            pe.sem_inc(one_hot_used, 4)
            with pe.Fori(0, TOPK * NT // 4) as i:
                for u in range(4):
                    pe.wait_ge(one_hot_ready, 4 * i + u + 1)
                    pe.matmul(ps_owner, at_row[:, u, :], at_tile[:, u, :], start=False, stop=False,
                              skip_group_check=True).then_inc(one_hot_used, 1)
            pe.matmul(ps_owner, before_bf[:], zero_bf[:], start=False, stop=True).then_inc(owner_ready, 1)
            pe.wait_ge(slots_ready, 1)
            pe.wait_ge(w_parts, 2 * E)

            def turn_x(j, u):
                b = u % 2
                pe.wait_ge(gathered[u], (j - u) * 4 + 16)
                wait(pe, xlo_ready, j - 1)
                for k in range(KD):
                    mm = pe.transpose(ps_xT[b][:, k, :], xg[:, u, k * P:(k + 1) * P], ident)
                mm.then_inc(xT_ready, 1)

            def gate_up(j, e, b):
                pe.wait_ge(xlo_ready, j + 1)
                wait(pe, h_ready, j - 1)
                n = 0
                for k in range(KD):
                    for x_part, w_part in ((xT_hi, gu_hi), (xT_hi, gu_lo), (xT_lo, gu_hi)):
                        n += 1
                        mm = pe.matmul(ps_gu[b][:], x_part[:, b, k, :], w_part[:, bass.ds(e, 1), k, :].rearrange("p a f -> p (a f)"),
                                       start=(n == 1), stop=(n == 3 * KD))
                mm.then_inc(gu_ready, 1)

            def turn_h(j, b):
                pe.wait_ge(h_ready, j + 1)
                wait(pe, hlo_ready, j - 1)
                for c in range(2):
                    mm = pe.transpose(ps_hT[b][:, c, :], h[:, b, c * FH:(c + 1) * FH], ident)
                mm.then_inc(hT_ready, 1)

            def down(j, e, b):
                pe.wait_ge(hlo_ready, j + 1)
                wait(pe, y_out, j - 1)
                n = 0
                for c in range(2):
                    for h_part, w_part in ((hT_hi, dn_hi), (hT_hi, dn_lo), (hT_lo, dn_hi)):
                        n += 1
                        mm = pe.matmul(ps_y[b][:], h_part[:, b, c, :], w_part[:, bass.ds(e, 1), c, :].rearrange("p a f -> p (a f)"),
                                       start=(n == 1), stop=(n == 6))
                mm.then_inc(y_ready, 1)

            def experts(first, n):
                _, values = nc.values_load_multi_w_load_instructions(expert_of[0:1, bass.ds(first, n)], engines=[mybir.EngineType.PE],
                                                                     min_val=0, max_val=E - 1)
                return values

            def steps(j, u, e):
                b = u % 2
                if is_tile(j):
                    gate_up(j, e[0], b)
                if is_tile(j - 1):
                    turn_h(j - 1, 1 - b)
                if is_tile(j + 2):
                    turn_x(j + 2, (u + 2) % 4)
                if is_tile(j - 2):
                    down(j - 2, e[1], b)

            turn_x(0, 0)
            turn_x(1, 1)
            for first in (0, 4):
                e = experts(first - min(first, 2), 4 + min(first, 2))
                for u in range(4):
                    at = u + min(first, 2)
                    steps(first + u, u, (e[at], e[at - 2] if at >= 2 else None))
            with pe.Fori(2, SLOT_TILES // 4 - 1) as i:
                e = experts(4 * i - 2, 6)
                for u in range(4):
                    steps(4 * i + u, u, (e[u + 2], e[u]))
            first = 4 * (SLOT_TILES // 4 - 1)
            e = experts(first - 2, SLOT_TILES - first + 2) + (None, None)
            for j in range(first, SLOT_TILES + 2):
                steps(j, j % 4, (e[j - first + 2], e[j - first]))


def known(n, *values):
    return isinstance(n, int) and n in values


def wait(eng, semaphore, value):
    if not isinstance(value, int) or value > 0:
        eng.wait_ge(semaphore, value)


def projection_phase(nc, cst, x_sb, v_sb, qkv_hi, qkv_lo, qk_dram):
    ctx = ExitStack()
    with Semaphores(nc) as sems, ctx:
        def sb(name, shape, dt=F32):
            return ctx.enter_context(nc.sbuf_tensor(f"p_{name}", shape, dt))

        def pb(name, shape, dt=F32):
            return ctx.enter_context(nc.psum_tensor(f"p_{name}", shape, dt))

        def sem(name):
            return sems.new(f"p_{name}")

        QK = 2 * D
        stats = sb("stats", [P, 8, 6])
        mv = sb("mv", [P, 8, 2])
        rstd = sb("rstd", [P, NT])
        nmr = sb("nmr", [P, NT])
        minus_half = sb("minus_half", [P, 8])
        xn = sb("xn", [P, 2, D])
        xT_hi = sb("xT_hi", [P, 2, KD, P], F32R)
        xT_lo = sb("xT_lo", [P, 2, KD, P], F32R)
        by_cos = sb("by_cos", [P, 2, QK])
        by_sin = sb("by_sin", [P, 2, QK])
        roped = sb("roped", [P, 2, QK])
        rT_hi = sb("rT_hi", [P, 2, 2 * KD, 2 * P], BF16)
        rT_mid = sb("rT_mid", [P, 2, 2 * KD, 2 * P], BF16)
        rT_lo = sb("rT_lo", [P, 2, 2 * KD, 2 * P], BF16)
        rT_rest = sb("rT_rest", [P, 2, 2 * KD, P])
        ps_xT = [pb(f"ps_xT{i}", [P, KD, P]) for i in range(2)]
        ps_qk = [pb(f"ps_qk{i}", [P, QK]) for i in range(2)]
        ps_v = [pb(f"ps_v{i}", [P, D]) for i in range(2)]
        ps_rT = [pb(f"ps_rT{i}", [P, 2 * KD, P]) for i in range(2)]
        stats_own, variances, pool_own, moments = sem("stats_own"), sem("variances"), sem("pool_own"), sem("moments")
        xn_ready, xT_ready, xhi_ready, xlo_ready = sem("xn_ready"), sem("xT_ready"), sem("xhi_ready"), sem("xlo_ready")
        qkv_ready, v_out, angled, roped_ready = sem("qkv_ready"), sem("v_out"), sem("angled"), sem("roped_ready")
        rT_ready, rhi_ready, rest_ready, rmid_ready, rlo_ready = (
            sem("rT_ready"), sem("rhi_ready"), sem("rest_ready"), sem("rmid_ready"), sem("rlo_ready"))
        stored = [sem(f"stored{i}") for i in range(2)]
        block = ctx.enter_context(nc.Block())

        def tiles(eng, step):
            for t in range(4):
                step(t, t)
            with eng.Fori(1, NT // 4 - 1) as i:
                for u in range(4):
                    step(4 * i + u, u)
            for u in range(4):
                step(NT - 4 + u, u)

        def beside(rT, u):
            return rT[:, u // 2, :, P * (u % 2):P * (u % 2) + P]

        @block.sync
        def _(sp):
            with sp.Fori(0, B) as b:
                with sp.Fori(0, TB // 4) as i:
                    for u in range(2):
                        sp.wait_ge(rlo_ready, 8 * b + 4 * i + 2 * u + 2)
                        for part, rT in enumerate((rT_hi, rT_mid, rT_lo)):
                            to = qk_dram[part, bass.ds(b, 1), :, :, bass.ds(2 * P * (2 * i + u), 2 * P)]
                            sp.dma_start(to.rearrange("b c r s -> (b r) c s"), rT[:, u, :, :]).then_inc(stored[u], 16)
            for u in range(2):
                sp.wait_ge(stored[u], 48 * (NT // 4))

        @block.gpsimd
        def _(pool):
            own = Own(pool, pool_own)
            own.then_wait(pool.memset(minus_half[:], -0.5))
            for g in range(4):
                q = slice(8 * g, 8 * g + 8)
                pool.wait_ge(variances, g + 1)
                own.then_wait(pool.tensor_tensor(rstd[:, q], rstd[:, q], minus_half[:], ALU.pow))
                pool.tensor_tensor(nmr[:, q], nmr[:, q], rstd[:, q], ALU.mult).then_inc(moments, 1)

            def r_low(t, u):
                pool.wait_ge(rmid_ready, t + 1)
                pool.tensor_tensor(beside(rT_lo, u), rT_rest[:, u % 2, :, :], beside(rT_mid, u), ALU.subtract).then_inc(rlo_ready, 1)

            def step(t, u):
                b = u % 2
                pool.wait_ge(angled, t + 1)
                wait(pool, rT_ready, t - 1)
                pool.tensor_tensor(roped[:, b, :].rearrange("p (a j h) -> p a h j", j=HD, h=HG),
                                   by_cos[:, b, :].rearrange("p (a h j) -> p a h j", j=HD, h=HG),
                                   by_sin[:, b, :].rearrange("p (a h j) -> p a h j", j=HD, h=HG), ALU.add).then_inc(roped_ready, 1)
                if not known(t, 0, 1):
                    r_low(t - 2, (u + 2) % 4)

            tiles(pool, step)
            r_low(NT - 2, 2)
            r_low(NT - 1, 3)

        @block.vector
        def _(dve):
            own = Own(dve, stats_own)
            with dve.Fori(0, NT // 8) as i:
                own.n = i * 16
                for u in range(8):
                    own.inc(dve.bn_stats(stats[:, u, :], x_sb[:, 8 * i + u, :]))
                own.wait()
                alone(dve)
                for u in range(8):
                    own.inc(dve.bn_aggr(mv[:, u, :], stats[:, u, :]))
                own.wait()
                dve.tensor_scalar(rstd[:, bass.ds(8 * i, 8)], mv[:, :, 1], EPS, None, ALU.add)
                dve.tensor_scalar(nmr[:, bass.ds(8 * i, 8)], mv[:, :, 0], -1.0, None, ALU.mult).then_inc(variances, 1)

            def x_low(t, b):
                dve.wait_ge(xhi_ready, t + 1)
                wait(dve, qkv_ready, t - 1)
                dve.tensor_tensor(xT_lo[:, b, :, :], ps_xT[b][:], xT_hi[:, b, :, :].bitcast(F32), ALU.subtract).then_inc(xlo_ready, 1)

            def turn_angles(t, b):
                dve.wait_ge(qkv_ready, t + 1)
                wait(dve, roped_ready, t - 1)
                halves = [P, 2 * NH, HD]
                cos = cst("cos").rearrange("p (t d) -> p t d", d=HD)[:, bass.ds(t, 1), :].to_broadcast(halves)
                sin = cst("sin").rearrange("p (t d) -> p t d", d=HD)[:, bass.ds(t, 1), :].to_broadcast(halves)
                x = ps_qk[b][:].rearrange("p (h d) -> p h d", d=HD)
                dve.tensor_tensor(by_cos[:, b, :].rearrange("p (h d) -> p h d", d=HD), x, cos, ALU.mult)
                y = by_sin[:, b, :].rearrange("p (h d) -> p h d", d=HD)
                dve.tensor_tensor(y[:, :, 0:HD // 2], x[:, :, HD // 2:HD], sin[:, :, 0:HD // 2], ALU.mult)
                dve.tensor_tensor(y[:, :, HD // 2:HD], x[:, :, 0:HD // 2], sin[:, :, HD // 2:HD], ALU.mult).then_inc(angled, 1)

            def rest(t, u):
                dve.wait_ge(rhi_ready, t + 1)
                wait(dve, rlo_ready, t - 1)
                dve.tensor_tensor(rT_rest[:, u % 2, :, :], ps_rT[u % 2][:], beside(rT_hi, u), ALU.subtract).then_inc(rest_ready, 1)

            def step(t, u):
                if not known(t, NT - 1):
                    x_low(t + 1, (u + 1) % 2)
                turn_angles(t, u % 2)
                if not known(t, 0):
                    rest(t - 1, (u + 3) % 4)

            x_low(0, 0)
            tiles(dve, step)
            rest(NT - 1, 3)

        @block.scalar
        def _(act):
            def normalise(t, b):
                act.wait_ge(moments, (t // 8) + 1)
                wait(act, xT_ready, t - 1)
                act.activation(xn[:, b, :], x_sb[:, t, :], ACT.Identity, bias=nmr[:, bass.ds(t, 1)], scale=rstd[:, bass.ds(t, 1)]).then_inc(xn_ready, 1)

            def x_high(t, b):
                act.wait_ge(xT_ready, t + 1)
                wait(act, qkv_ready, t - 1)
                act.activation(xT_hi[:, b, :, :], ps_xT[b][:], ACT.Copy).then_inc(xhi_ready, 1)

            def v_copy(t, b):
                act.wait_ge(qkv_ready, t + 1)
                act.activation(v_sb[:, bass.ds(t // TB, 1), :, bass.ds(t % TB, 1), :].rearrange("p b g t d -> p (b t) g d"),
                               ps_v[b][:].rearrange("p (a g d) -> p a g d", a=1, g=NG), ACT.Copy).then_inc(v_out, 1)

            def r_high(t, u):
                act.wait_ge(rT_ready, t + 1)
                if u % 2 == 0:
                    wait(act, stored[u // 2], 12 * (t - u))
                act.activation(beside(rT_hi, u), ps_rT[u % 2][:], ACT.Copy).then_inc(rhi_ready, 1)

            def r_mid(t, u):
                act.wait_ge(rest_ready, t + 1)
                act.activation(beside(rT_mid, u), rT_rest[:, u % 2, :, :], ACT.Copy).then_inc(rmid_ready, 1)

            def step(t, u):
                b = u % 2
                if not known(t, NT - 2, NT - 1):
                    normalise(t + 2, b)
                if not known(t, NT - 1):
                    x_high(t + 1, 1 - b)
                v_copy(t, b)
                if not known(t, 0):
                    r_high(t - 1, (u + 3) % 4)
                if not known(t, 0, 1):
                    r_mid(t - 2, (u + 2) % 4)

            normalise(0, 0)
            normalise(1, 1)
            x_high(0, 0)
            tiles(act, step)
            r_high(NT - 1, 3)
            r_mid(NT - 2, 2)
            r_mid(NT - 1, 3)

        @block.tensor
        def _(pe):
            ident = cst("ident")

            def turn_x(t, b):
                pe.wait_ge(xn_ready, t + 1)
                wait(pe, xlo_ready, t - 1)
                for k in range(KD):
                    mm = pe.transpose(ps_xT[b][:, k, :], xn[:, b, k * P:(k + 1) * P], ident)
                mm.then_inc(xT_ready, 1)

            def project(t, b):
                pe.wait_ge(xlo_ready, t + 1)
                wait(pe, angled, t - 1)
                wait(pe, v_out, t - 1)
                n = 0
                for k in range(KD):
                    for x_part, w_part in ((xT_hi, qkv_hi), (xT_hi, qkv_lo), (xT_lo, qkv_hi)):
                        n += 1
                        pe.matmul(ps_qk[b][:], x_part[:, b, k, :], w_part[:, k, 0:QK], start=(n == 1), stop=(n == 3 * KD))
                        mm = pe.matmul(ps_v[b][:], x_part[:, b, k, :], w_part[:, k, QK:QK + D], start=(n == 1), stop=(n == 3 * KD))
                mm.then_inc(qkv_ready, 1)

            def turn_r(t, b):
                pe.wait_ge(roped_ready, t + 1)
                wait(pe, rest_ready, t - 1)
                for c in range(2 * KD):
                    mm = pe.transpose(ps_rT[b][:, c, :], roped[:, b, c * P:(c + 1) * P], ident)
                mm.then_inc(rT_ready, 1)

            def step(t, u):
                b = u % 2
                if not known(t, NT - 1):
                    turn_x(t + 1, 1 - b)
                project(t, b)
                if not known(t, 0):
                    turn_r(t - 1, 1 - b)

            turn_x(0, 0)
            tiles(pe, step)
            turn_r(NT - 1, 1)


UNITS1 = [(h, i, k0, n) for h in range(HG) for i in range(TB)
          for k0, n in ([(0, P * (i + 1))] if i < TB // 2 else [(0, HALF), (HALF, P * (i + 1) - HALF)])]
UNITS2 = [(half, j, max(HALF * half, P * j), HALF * (half + 1) - max(HALF * half, P * j), pair)
          for half in range(2) for j in range(4 * half + 4) for pair in range(2)]
N1, N2, NV = len(UNITS1), len(UNITS2), len(UNITS2) // 2
CUTS = [n for n, (half, j, _, _, _) in enumerate(UNITS2) if j >= 4 * half]
LAG = 3
TERMS = [(0, 0), (0, 1), (0, 2), (1, 0), (1, 1), (2, 0)]
MAX_ROW = len(TERMS) * HD
ROWS = MAX_ROW + 2


def first_pass_schedule():
    done = sum(nq for _, _, _, nq, _ in UNITS2[:MAX_STEP])
    total, all_keys = sum(nq for _, _, _, nq, _ in UNITS2), sum(n for _, _, _, n in UNITS1)
    at = all_keys * (1 - done / total)
    r, keys, ahead, steps = 0, 0, 1, []
    while keys < at:
        keys += UNITS1[r][3]
        r += 1
    early = r
    for s, (_, _, _, nq, _) in enumerate(UNITS2):
        at += nq * all_keys / total
        units = []
        while keys < at - 1e-6 and (ahead == 1 or r < early):
            units.append((ahead, r))
            keys += UNITS1[r][3]
            r += 1
            if r == N1:
                r, ahead = 0, 2
        steps.append(units)
    while r < early:
        steps[-1].append((2, r))
        r += 1
    return steps, early


SPLIT = 2
MAX_STEP = 16
STEPS, EARLY = first_pass_schedule()
assert sum(len(u) for u in STEPS) == N1
MAX_STEP = [s for s, u in enumerate(STEPS) if (1, N1 - 1) in u][0]
PASSED = [[("scores", ahead, r) for ahead, r in units] for units in STEPS]
PASSED[LAG + 1].append(("sums", -1, 1))
PASSED[12].append(("sums", 0, 0))
PASSED[MAX_STEP + 2].append(("maxima", 1, 0))
PER_GROUP = sum(len(x) for x in PASSED)
assert PER_GROUP % 3 == 0 and MAX_STEP + 4 < N2


def attention_phase(nc, cst, v_sb, qk_dram):
    ctx = ExitStack()
    with Semaphores(nc) as sems, ctx:
        def sb(name, shape, dt=F32):
            return ctx.enter_context(nc.sbuf_tensor(f"a_{name}", shape, dt))

        def pb(name, shape, dt=F32):
            return ctx.enter_context(nc.psum_tensor(f"a_{name}", shape, dt))

        def sem(name):
            return sems.new(f"a_{name}")

        RING = 4
        q_st = [sb(f"q_st{i}", [ROWS, HG, S], BF16) for i in range(RING)]
        k_st = [sb(f"k_st{i}", [ROWS, HG, S], BF16) for i in range(RING)]
        v_st = [sb(f"v_st{i}", [P, TB, HG, 2 * HD]) for i in range(2)]
        zeros = sb("zeros", [HG * TB, P], BF16)
        probs = sb("probs", [P, 4, 2, HALF])
        unused = sb("unused", [P, 3, HALF], BF16)
        max_a = sb("max_a", [P, 2, HG, TB])
        max_b = sb("max_b", [P, 2, HG, TB // 2])
        max_row = sb("max_row", [HG * TB, 2, P], BF16)
        ctxT = sb("ctxT", [P, 2, HALF])
        recip = sb("recip", [P, 2, 4, HG])
        ps_s = [pb(f"ps_s{i}", [P, 2, HALF]) for i in range(2)]
        ps_m = [pb(f"ps_m{i}", [P, HALF]) for i in range(3)]
        ps_ctx = pb("ps_ctx", [P, HALF])
        inits, padded = sem("inits"), sem("padded")
        stack_in = [sem(f"stack_in{i}") for i in range(RING)]
        max_in = [sem(f"max_in{i}") for i in range(RING)]
        v_copied, max_high = sem("v_copied"), sem("max_high")
        scored, exp_done, cut_done, pv_done = sem("scored"), sem("exp_done"), sem("cut_done"), sem("pv_done")
        passed, taken, max_ready, max_row_ready = sem("passed"), sem("taken"), sem("max_ready"), sem("max_row_ready")
        ctx_out, ctx_turned, recip_ready = sem("ctx_out"), sem("ctx_turned"), sem("recip_ready")
        block = ctx.enter_context(nc.Block())
        NGR = B * NG
        LOADS = 16 * (2 * len(TERMS) + 2)

        def groups(eng, group):
            group(0, 0)
            with eng.Fori(0, NGR // RING - 1) as i:
                for r in range(RING):
                    group(RING * i + r + 1, (r + 1) % RING)
            for g in range(NGR - 3, NGR):
                group(g, g % RING)

        def is_last(g):
            return isinstance(g, int) and g == NGR - 1

        def exists(g):
            return not isinstance(g, int) or 0 <= g < NGR

        def is_first(g):
            return isinstance(g, int) and g == 0

        BEFORE = N1 + 1 + EARLY

        def passed_before(g):
            if isinstance(g, int):
                return BEFORE + sum(exists(p + ahead) for p in range(g) for x in PASSED for _, ahead, _ in x)
            return (g - 1) * PER_GROUP + BEFORE + PER_GROUP - 1

        TOTAL = passed_before(NGR)

        def passed_in(g):
            number = passed_before(g)
            bank = number if isinstance(g, int) else passed_before(1)
            k, steps = 0, []
            for x in PASSED:
                steps.append([])
                for kind, ahead, r in x:
                    if exists(g + ahead):
                        steps[-1].append((kind, ahead, r, number + k, (bank + k) % 3))
                        k += 1
            return steps

        @block.sync
        def _(sp):
            def row_of_max(b, part):
                return q_st[b][MAX_ROW + part:MAX_ROW + part + 1, :, :].rearrange("o h (i s) -> o (h i) s", s=P)

            def load(g, b):
                for qk, stack in ((0, q_st[b]), (1, k_st[b])):
                    for r, term in enumerate(TERMS):
                        src = qk_dram[term[qk]].rearrange("b c (f r) s -> (b c f) r s", f=2)[bass.ds((g // NG) * 2 * NG + g % NG + qk * NG, 1), :, :]
                        sp.dma_start(stack[HD * r:HD * r + HD, :, :], src.rearrange("o (j h) s -> (o j) h s", j=HD)).then_inc(stack_in[b], 16)
                for part in range(2):
                    sp.dma_start(row_of_max(b, part), zeros[:]).then_inc(stack_in[b], 16)

            def send_max(g, b):
                sp.wait_ge(max_row_ready, g + 1)
                for part in range(2):
                    sp.dma_start(row_of_max(b, part), max_row[:, part, :]).then_inc(max_in[b], 16)

            sp.wait_ge(inits, 1)
            for g in range(RING - 1):
                load(g, g)
            send_max(0, 0)

            def group(g, b):
                if not (isinstance(g, int) and g > NGR - RING):
                    wait(sp, scored, N2 * g)
                    load(g + RING - 1, (b + RING - 1) % RING)
                if not is_last(g):
                    send_max(g + 1, (b + 1) % RING)

            groups(sp, group)

        @block.gpsimd
        def _(pool):
            pool.memset(zeros[:], 0.0).then_inc(inits, 1)

            def copy_v(g, b):
                wait(pool, pv_done, NV * (g - 1))
                pool.tensor_copy(v_st[b % 2][:, :, :, 0:HD],
                                 v_sb[:].rearrange("p b g t d -> p (b g) t d")[:, bass.ds(g, 1), :, :]
                                 .rearrange("p o t (h d) -> p (o t) h d", d=HD)).then_inc(v_copied, 1)

            copy_v(0, 0)
            zero = pool.to_reg(0.0)

            def group(g, b):
                for c, n in enumerate(CUTS):
                    pool.wait_ge(exp_done, N2 * g + n + 1)
                    tri = probs[:, n % 4, :, 0:P]
                    alone(pool)
                    pool.affine_select(out=tri, in_=tri, compare_op=ALU.is_ge, fill=zero, base=0, pattern=[[0, 2], [1, P]],
                                       channel_multiplier=-1).then_inc(cut_done, 1)
                    if c == 8 and not is_last(g):
                        copy_v(g + 1, (b + 1) % 2)

            groups(pool, group)

        @block.vector
        def _(dve):
            def read_unit(b, r, n, bank):
                h, i, k0, nk = UNITS1[r]
                dve.wait_ge(passed, n + 1)
                if not known(n, 0, 1, 2):
                    dve.wait_ge(taken, n - 2)
                alone(dve)
                ps = ps_m[bank][:, 0:nk]
                at = max_a[:, b % 2, h, i:i + 1] if k0 == 0 else max_b[:, b % 2, h, i - 4:i - 3]
                if k0 + nk == P * (i + 1):
                    dve.tensor_tensor_reduce(unused[:, bank, 0:nk], ps, cst("mask")[:, HALF - nk:HALF], 1.0, NEG, ALU.add, ALU.max, at).then_inc(taken, 1)
                else:
                    dve.tensor_reduce(at, ps, AX.X, ALU.max).then_inc(taken, 1)
                if r == N1 - 1:
                    dve.wait_ge(taken, n + 1)
                    late = max_a[:, b % 2, :, TB // 2:TB]
                    dve.tensor_tensor(late, late, max_b[:, b % 2, :, :], ALU.max).then_inc(max_ready, 1)

            def rows_of_max(g, n, bank):
                dve.wait_ge(passed, n + 1)
                turned = ps_m[bank][0:HG * TB, 0:P]
                dve.tensor_scalar(max_row[:, 0, :], turned, -1.0, None, ALU.mult).then_inc(max_high, 1)
                dve.wait_ge(max_high, g + 1)
                dve.scalar_tensor_tensor(max_row[:, 1, :], turned, -1.0, max_row[:, 0, :], ALU.mult, ALU.subtract).then_inc(taken, 1)
                dve.wait_ge(taken, n + 1)
                dve.sem_inc(max_row_ready, 1)

            def divide(g, half, n, bank):
                dve.wait_ge(passed, n + 1)
                sums = ps_m[bank][:].rearrange("p (i h d) -> p i h d", i=4, h=HG)
                dve.wait_ge(taken, n - 1)
                dve.reciprocal(recip[:, half, :, :], sums[:, :, :, HD]).then_inc(recip_ready, 1)
                dve.wait_ge(recip_ready, 2 * g + half + 1)
                to = v_sb[:].rearrange("p b g t d -> p (b g) t d")[:, bass.ds(g, 1), 4 * half:4 * half + 4, :]
                to = to.rearrange("p o t (h d) -> p (o t) h d", d=HD)
                dve.tensor_tensor(to, sums[:, :, :, 0:HD], recip[:, half, :, :].unsqueeze(3).to_broadcast([P, 4, HG, HD]), ALU.mult).then_inc(taken, 1)

            for b in range(RING):
                dve.memset(k_st[b][MAX_ROW:ROWS, :, :], 1.0).then_inc(padded, 1)
            for b in range(2):
                dve.memset(v_st[b][:, :, :, HD:HD + 1], 1.0)
                dve.memset(v_st[b][:, :, :, HD + 1:2 * HD], 0.0).then_inc(padded, 1)
            for r in range(N1):
                read_unit(0, r, r, r % 3)
            rows_of_max(0, N1, N1 % 3)
            for r in range(EARLY):
                read_unit(1, r, N1 + 1 + r, (N1 + 1 + r) % 3)

            def group(g, b):
                for step in passed_in(g):
                    for kind, ahead, r, n, bank in step:
                        if kind == "scores":
                            read_unit((b + ahead) % RING, r, n, bank)
                        elif kind == "sums":
                            divide(g + ahead, r, n, bank)
                        else:
                            rows_of_max(g + ahead, n, bank)

            groups(dve, group)
            divide(NGR - 1, 1, TOTAL, TOTAL % 3)

        @block.scalar
        def _(act):
            def evacuate(g, half, before):
                act.wait_ge(pv_done, NV * g + 4 + 8 * half)
                act.wait_ge(passed, before)
                act.activation(ctxT[:, half, :], ps_ctx[:], ACT.Copy).then_inc(ctx_out, 1)

            def group(g, b):
                for s, (half, j, q0, nq, pair) in enumerate(UNITS2):
                    if s == 2 and not is_first(g):
                        evacuate(g - 1, 1, passed_before(g))
                    if s == 10:
                        evacuate(g, 0, passed_before(g))
                    act.wait_ge(scored, N2 * g + s + 1)
                    if not (is_first(g) and s < 4):
                        act.wait_ge(pv_done, NV * g + s // 2 - 1)
                    act.activation(probs[:, s % 4, :, 0:nq], ps_s[s % 2][:, :, 0:nq], ACT.Exp, scale=float(HD) ** -0.5).then_inc(exp_done, 1)

            groups(act, group)
            evacuate(NGR - 1, 1, TOTAL)

        @block.tensor
        def _(pe):
            ident = cst("ident")

            def free(n):
                if not known(n, 0, 1, 2):
                    pe.wait_ge(taken, n - 2)

            def first_unit(b, r, n, bank):
                h, i, k0, nk = UNITS1[r]
                free(n)
                pe.matmul(ps_m[bank][:, 0:nk], q_st[b][:, h, P * i:P * i + P], k_st[b][:, h, k0:k0 + nk],
                          start=True, stop=True).then_inc(passed, 1)

            def turn_max(g, b, n, bank):
                free(n)
                pe.wait_ge(max_ready, g + 1)
                pe.transpose(ps_m[bank][0:HG * TB, 0:P], max_a[:, b % 2, :, :].rearrange("p h i -> p (h i)"), ident).then_inc(passed, 1)

            def second_unit(g, b, s):
                half, j, q0, nq, pair = UNITS2[s]
                if not (is_first(g) and s < 2):
                    pe.wait_ge(exp_done, N2 * g + s - 1)
                for n in range(2):
                    h = 2 * pair + n
                    mm = pe.matmul(ps_s[s % 2][:, n, 0:nq], k_st[b][:, h, P * j:P * j + P], q_st[b][:, h, q0:q0 + nq],
                                   start=True, stop=True)
                mm.then_inc(scored, 1)

            def times_v(g, b, v):
                half, j, q0, nq, _ = UNITS2[2 * v]
                pe.wait_ge(exp_done, N2 * g + 2 * v + 2)
                if 2 * v in CUTS:
                    pe.wait_ge(cut_done, len(CUTS) * g + CUTS.index(2 * v) + 2)
                if j == 0:
                    wait(pe, ctx_out, 2 * g + half)
                for h in range(HG):
                    mm = pe.matmul(ps_ctx[32 * h:32 * h + 32, q0 - HALF * half:HALF], v_st[b % 2][:, j, h, :],
                                   probs[:, (2 * v + h // 2) % 4, h % 2, 0:nq], start=(j == 0), stop=(j == 4 * half + 3),
                                   skip_group_check=True)
                mm.then_inc(pv_done, 1)

            def turn_ctx(g, half, n, bank):
                free(n)
                pe.wait_ge(ctx_out, 2 * g + half + 1)
                for i in range(4):
                    mm = pe.transpose(ps_m[bank][:, P * i:P * i + P], ctxT[:, half, P * i:P * i + P], ident)
                mm.then_inc(passed, 1)

            pe.wait_ge(padded, RING + 2)
            pe.wait_ge(stack_in[0], LOADS)
            for r in range(N1):
                first_unit(0, r, r, r % 3)
            turn_max(0, 0, N1, N1 % 3)
            pe.wait_ge(stack_in[1], LOADS)
            for r in range(EARLY):
                first_unit(1, r, N1 + 1 + r, (N1 + 1 + r) % 3)

            def group(g, b):
                def pass_on(step):
                    for kind, ahead, r, n, bank in step:
                        to = (b + ahead) % RING
                        if kind == "scores":
                            if r == 0:
                                pe.wait_ge(stack_in[to], turns(g + ahead, to) * LOADS)
                            first_unit(to, r, n, bank)
                        elif kind == "sums":
                            turn_ctx(g + ahead, r, n, bank)
                        else:
                            turn_max(g + ahead, to, n, bank)

                for s, step in enumerate(passed_in(g)):
                    if s == 0:
                        pe.wait_ge(max_in[b], turns(g, b) * 32)
                    second_unit(g, b, s)
                    if s == 1 and not is_first(g):
                        times_v(g - 1, (b - 1) % RING, NV - 1)
                    pass_on(step[:SPLIT])
                    if s % 2 == 1 and s >= LAG:
                        if s == LAG:
                            pe.wait_ge(v_copied, g + 1)
                        times_v(g, b, (s - LAG) // 2)
                    pass_on(step[SPLIT:])

            def turns(g, b):
                if isinstance(g, int):
                    return g // RING + 1
                return (g - b) // RING + 1

            groups(pe, group)
            times_v(NGR - 1, (NGR - 1) % RING, NV - 1)
            turn_ctx(NGR - 1, 1, TOTAL, TOTAL % 3)


def output_phase(nc, cst, x_sb, v_sb, wo_hi, wo_lo, out):
    ctx = ExitStack()
    with Semaphores(nc) as sems, ctx:
        def sb(name, shape, dt=F32):
            return ctx.enter_context(nc.sbuf_tensor(f"o_{name}", shape, dt))

        def pb(name, shape, dt=F32):
            return ctx.enter_context(nc.psum_tensor(f"o_{name}", shape, dt))

        def sem(name):
            return sems.new(f"o_{name}")

        cx = sb("cx", [P, 2, D])
        cT_hi = sb("cT_hi", [P, 2, KD, P], F32R)
        cT_lo = sb("cT_lo", [P, 2, KD, P], F32R)
        ps_cT = [pb(f"ps_cT{i}", [P, KD, P]) for i in range(2)]
        ps_o = [pb(f"ps_o{i}", [P, D]) for i in range(2)]
        cx_ready, cT_ready, chi_ready, clo_ready, o_ready, summed = (
            sem("cx_ready"), sem("cT_ready"), sem("chi_ready"), sem("clo_ready"), sem("o_ready"), sem("summed"))
        out_stored = sem("out_stored")
        block = ctx.enter_context(nc.Block())

        def tiles(eng, step):
            for t in range(4):
                step(t, t % 2)
            with eng.Fori(2, NT // 2) as i:
                for u in range(2):
                    step(2 * i + u, u)

        @block.sync
        def _(sp):
            if out is not None:
                sp.wait_ge(summed, NT)
                sp.dma_start(out.rearrange("(t p) d -> p t d", p=P), x_sb[:]).then_inc(out_stored, 16)
                sp.wait_ge(out_stored, 16)

        @block.gpsimd
        def _(pool):
            def step(t, b):
                wait(pool, cT_ready, t - 1)
                pool.tensor_copy(cx[:, b, :].rearrange("p (a g d) -> p a g d", a=1, g=NG),
                                 v_sb[:, bass.ds(t // TB, 1), :, bass.ds(t % TB, 1), :].rearrange("p b g t d -> p (b t) g d")).then_inc(cx_ready, 1)

            tiles(pool, step)

        @block.tensor
        def _(pe):
            def turn(t, b):
                pe.wait_ge(cx_ready, t + 1)
                wait(pe, clo_ready, t - 1)
                for k in range(KD):
                    mm = pe.transpose(ps_cT[b][:, k, :], cx[:, b, k * P:(k + 1) * P], cst("ident"))
                mm.then_inc(cT_ready, 1)

            def product(t, b):
                pe.wait_ge(clo_ready, t + 1)
                wait(pe, summed, t - 1)
                n = 0
                for k in range(KD):
                    for c_part, w_part in ((cT_hi, wo_hi), (cT_hi, wo_lo), (cT_lo, wo_hi)):
                        n += 1
                        mm = pe.matmul(ps_o[b][:], c_part[:, b, k, :], w_part[:, k, :], start=(n == 1), stop=(n == 3 * KD))
                mm.then_inc(o_ready, 1)

            def step(t, b):
                turn(t, b)
                if not (isinstance(t, int) and t == 0):
                    product(t - 1, 1 - b)

            tiles(pe, step)
            product(NT - 1, 1)

        @block.scalar
        def _(act):
            def step(t, b):
                act.wait_ge(cT_ready, t + 1)
                wait(act, o_ready, t - 1)
                act.activation(cT_hi[:, b, :, :], ps_cT[b][:], ACT.Copy).then_inc(chi_ready, 1)

            tiles(act, step)

        @block.vector
        def _(dve):
            def low(t, b):
                dve.wait_ge(chi_ready, t + 1)
                wait(dve, o_ready, t - 1)
                dve.tensor_tensor(cT_lo[:, b, :, :], ps_cT[b][:], cT_hi[:, b, :, :].bitcast(F32), ALU.subtract).then_inc(clo_ready, 1)

            def add(t, b):
                dve.wait_ge(o_ready, t + 1)
                dve.tensor_tensor(x_sb[:, t, :], ps_o[b][:], x_sb[:, t, :], ALU.add).then_inc(summed, 1)

            def step(t, b):
                low(t, b)
                if not (isinstance(t, int) and t == 0):
                    add(t - 1, 1 - b)

            tiles(dve, step)
            add(NT - 1, 1)


def setup_phase(nc, consts, x, gate_w, wq, wk, wv, wo, const_sb, x_sb, gate_sb, qkv_hi, qkv_lo, wo_hi, wo_lo):
    ctx = ExitStack()
    with ctx:
        raw = ctx.enter_context(nc.sbuf_tensor("s_raw", [P, 4, 2, D], F32))
        gate_raw = ctx.enter_context(nc.sbuf_tensor("s_gate_raw", [E, D], F32))
        ps = [ctx.enter_context(nc.psum_tensor(f"s_ps{i}", [P, 2, 2, P], F32)) for i in range(4)]
        ps_gate = ctx.enter_context(nc.psum_tensor("s_ps_gate", [P, KD, E], F32))
        consts_in = ctx.enter_context(nc.semaphore("s_consts_in"))
        w_in = [ctx.enter_context(nc.semaphore(f"s_w_in{i}")) for i in range(5)]
        x_in = ctx.enter_context(nc.semaphore("s_x_in"))
        turned = ctx.enter_context(nc.semaphore("s_turned"))
        hi_done = ctx.enter_context(nc.semaphore("s_hi_done"))
        lo_done = ctx.enter_context(nc.semaphore("s_lo_done"))
        block = ctx.enter_context(nc.Block())

        def cst(name):
            at, w = CONST_AT[name]
            return const_sb[:, at:at + w]

        def parts(m):
            if m == 3:
                return wo_hi[:], wo_lo[:]
            return qkv_hi[:, :, m * D:(m + 1) * D], qkv_lo[:, :, m * D:(m + 1) * D]

        @block.sync
        def _(sp):
            sp.dma_start(const_sb[:], consts).then_inc(consts_in, 16)
            sp.dma_start(gate_raw[:], gate_w).then_inc(w_in[4], 16)
            for m, w in enumerate((wq, wk, wv, wo)):
                sp.dma_start(raw[:, m, :, :], w.rearrange("(c p) h -> p c h", p=P)).then_inc(w_in[m], 16)
            sp.wait_ge(x_in, 64)

        @block.scalar
        def _(act):
            for q in range(4):
                act.dma_start(x_sb[:, 8 * q:8 * q + 8, :], x[8 * q * P:8 * (q + 1) * P, :].rearrange("(t p) d -> p t d", p=P)).then_inc(x_in, 16)
            for m in range(4):
                act.wait_ge(turned, m + 2)
                act.activation(parts(m)[0].rearrange("p k (c o) -> p k c o", c=2), ps[m][:], ACT.Copy).then_inc(hi_done, 1)

        @block.tensor
        def _(pe):
            pe.wait_ge(consts_in, 16)
            pe.wait_ge(w_in[4], 16)
            for k in range(KD):
                mm = pe.transpose(ps_gate[:, k, :], gate_raw[:, k * P:(k + 1) * P], cst("ident")[0:E, 0:E])
            mm.then_inc(turned, 1)
            for m in range(4):
                pe.wait_ge(w_in[m], 16)
                for k in range(KD):
                    for c in range(2):
                        mm = pe.transpose(ps[m][:, k, c, :], raw[:, m, c, k * P:(k + 1) * P], cst("ident"))
                mm.then_inc(turned, 1)

        @block.vector
        def _(dve):
            dve.wait_ge(turned, 1)
            dve.tensor_copy(gate_sb[:], ps_gate[:])
            for m in range(4):
                dve.wait_ge(hi_done, m + 1)
                hi, lo = parts(m)
                dve.tensor_tensor(lo.rearrange("p k (c o) -> p k c o", c=2), ps[m][:],
                                  hi.bitcast(F32).rearrange("p k (c o) -> p k c o", c=2), ALU.subtract).then_inc(lo_done, 1)


def program(nc, consts, x, gate_w, w_gate, w_up, w_down, wq, wk, wv, wo, out, phases=("ffn1", "attn", "ffn2")):
    ctx = ExitStack()
    with ctx:
        def sb(name, shape, dt=F32):
            return ctx.enter_context(nc.sbuf_tensor(name, shape, dt))

        x = x.rearrange("b s d -> (b s) d")
        out = out.rearrange("b s d -> (b s) d")
        const_sb = sb("const_sb", [P, CONST_N])
        gate_sb = sb("gate_sb", [P, KD, E])
        qkv_hi, qkv_lo = (sb(f"qkv_{p}", [P, KD, 3 * D], F32R) for p in ("hi", "lo"))
        wo_hi, wo_lo = (sb(f"wo_{p}", [P, KD, D], F32R) for p in ("hi", "lo"))
        xn_dram = nc.dram_tensor("xn_dram", [T, D], F32, kind="Internal").ap()
        y_dram = nc.dram_tensor("y_dram", [T * TOPK, D], F32, kind="Internal").ap()
        qk_dram = nc.dram_tensor("qk_dram", [3, B, 2 * KD, P, S], BF16, kind="Internal").ap()

        def cst(name):
            at, w = CONST_AT[name]
            return const_sb[:, at:at + w]

        v_sb = sb("v_sb", [P, B, NG, TB, HG * HD])
        spare = v_sb[:].rearrange("p b g t d -> p (b g t d)")
        x_sb = sb("x_sb", [P, NT, D])
        setup_phase(nc, consts, x, gate_w, wq, wk, wv, wo, const_sb, x_sb, gate_sb, qkv_hi, qkv_lo, wo_hi, wo_lo)
        last = phases[-1]
        if "ffn1" in phases:
            ffn_phase(nc, "f1", cst, x_sb, gate_sb, w_gate, w_up, w_down, xn_dram, y_dram, spare, out if last == "ffn1" else None)
        if "attn" in phases:
            projection_phase(nc, cst, x_sb, v_sb, qkv_hi, qkv_lo, qk_dram)
            attention_phase(nc, cst, v_sb, qk_dram)
            output_phase(nc, cst, x_sb, v_sb, wo_hi, wo_lo, out if last == "attn" else None)
        if "ffn2" in phases:
            ffn_phase(nc, "f2", cst, x_sb, gate_sb, w_gate, w_up, w_down, xn_dram, y_dram, spare, out)


INPUTS = ["L0_attn_hidden_states", "L0_ffn_gate_w", "L0_ffn_w_gate", "L0_ffn_w_up", "L0_ffn_w_down",
          "L0_attn_Wq", "L0_attn_Wk", "L0_attn_Wv", "L0_attn_Wo"]


def kernel(**inputs):
    import concourse.bacc as bacc
    from concourse.bass_utils import run_bass_kernel_spmd

    nc = bacc.Bacc("TRN2", target_bir_lowering=False, num_devices=1)
    arrays = {"consts": constants()}
    arrays.update({name: np.ascontiguousarray(inputs[name]) for name in INPUTS})
    args = [nc.dram_tensor(name, a.shape, mybir.dt.from_np(a.dtype), kind="ExternalInput").ap() for name, a in arrays.items()]
    out = nc.dram_tensor("out", (B, S, D), F32, kind="ExternalOutput").ap()
    program(nc, *args, out)
    return run_bass_kernel_spmd(nc, [arrays], core_ids=[0]).results[0]["out"]
```
